# Optimizing a Trainium2 kernel written in Bass

```python
import numpy as np
import jax
import jax.numpy as jnp

def _softmax(x, axis=-1):
    return jax.nn.softmax(x, axis=axis)

def _gelu(x):
    return jax.nn.gelu(x, approximate=True)

def _silu(x):
    return jax.nn.silu(x)

def _sigmoid(x):
    return jax.nn.sigmoid(x)

def _layernorm(x, axis=-1, eps=1e-05):
    m = jnp.mean(x, axis=axis, keepdims=True)
    v = jnp.var(x, axis=axis, keepdims=True)
    return (x - m) / jnp.sqrt(v + eps)

def _scatter_add(tgt, idx, src, axis=0):
    return tgt.at[idx].add(src)

def _segment_sum(src, seg, n):
    return jax.ops.segment_sum(src, seg, n)
kernel_name = 'mk_sandwich_d1_jaxref_r4_be8301'

def setup_inputs(seed: int=0):
    np.random.seed(seed)
    _w = jnp.asarray

    def _L0_attn_setup():
        import jax, jax.numpy as jnp
        import numpy as np
        EMBED_DIM = 256
        NUM_HEAD = 16
        NEG_BIG = 10000000000.0
        key = jax.random.key(seed)
        k_x, k_w1, k_b1, k_w2, k_b2 = jax.random.split(key, 5)
        B, S, E = (4, 512, EMBED_DIM)
        std = 1.0 / np.sqrt(E)
        return {'x': jax.random.normal(k_x, (B, S, E), dtype=jnp.float32), 'W1': jax.random.uniform(k_w1, (E, 3 * E), dtype=jnp.float32, minval=-std, maxval=std), 'b1': jax.random.uniform(k_b1, (3 * E,), dtype=jnp.float32, minval=-std, maxval=std), 'W2': jax.random.uniform(k_w2, (E, E), dtype=jnp.float32, minval=-std, maxval=std), 'b2': jax.random.uniform(k_b2, (E,), dtype=jnp.float32, minval=-std, maxval=std)}
    _L0_attn_in = _L0_attn_setup()

    def _L0_ffn_setup():
        import jax, jax.numpy as jnp
        import numpy as np
        B, S, D = (2, 128, 256)
        E, K, I = (16, 8, 256)
        I_SH = 256
        ROUTE_SCALE = 2.826
        key = jax.random.key(seed)
        ks = jax.random.split(key, 8)
        s = 0.02
        return {'x': jax.random.normal(ks[0], (B, S, D), dtype=jnp.float32), 'gate_w': jax.random.normal(ks[1], (E, D), dtype=jnp.float32) * s, 'expert_bias': jnp.zeros((E,), dtype=jnp.float32), 'w_gate': jax.random.normal(ks[2], (E, I, D), dtype=jnp.float32) * s, 'w_up': jax.random.normal(ks[3], (E, I, D), dtype=jnp.float32) * s, 'w_down': jax.random.normal(ks[4], (E, D, I), dtype=jnp.float32) * s, 'shared_gate_w': jax.random.normal(ks[5], (I_SH, D), dtype=jnp.float32) * s, 'shared_up_w': jax.random.normal(ks[6], (I_SH, D), dtype=jnp.float32) * s, 'shared_down_w': jax.random.normal(ks[7], (D, I_SH), dtype=jnp.float32) * s}
    _L0_ffn_in = _L0_ffn_setup()
    _d = {'L0_attn_x': _L0_attn_in['x'], 'L0_attn_W1': _L0_attn_in['W1'], 'L0_attn_b1': _L0_attn_in['b1'], 'L0_attn_W2': _L0_attn_in['W2'], 'L0_attn_b2': _L0_attn_in['b2'], 'L0_ffn_gate_w': _L0_ffn_in['gate_w'], 'L0_ffn_expert_bias': _L0_ffn_in['expert_bias'], 'L0_ffn_w_gate': _L0_ffn_in['w_gate'], 'L0_ffn_w_up': _L0_ffn_in['w_up'], 'L0_ffn_w_down': _L0_ffn_in['w_down'], 'L0_ffn_shared_gate_w': _L0_ffn_in['shared_gate_w'], 'L0_ffn_shared_up_w': _L0_ffn_in['shared_up_w'], 'L0_ffn_shared_down_w': _L0_ffn_in['shared_down_w']}
    _x0 = _d['L0_attn_x']
    _d['L0_attn_x'] = jax.random.normal(jax.random.fold_in(jax.random.key(seed), 1), (8, 1024, 256), dtype=_x0.dtype)
    del _x0
    return _d

def reference(L0_attn_x, L0_attn_W1, L0_attn_b1, L0_attn_W2, L0_attn_b2, L0_ffn_gate_w, L0_ffn_expert_bias, L0_ffn_w_gate, L0_ffn_w_up, L0_ffn_w_down, L0_ffn_shared_gate_w, L0_ffn_shared_up_w, L0_ffn_shared_down_w):

    def _L0_attn_ref(x, W1, b1, W2, b2):
        import jax, jax.numpy as jnp
        import numpy as np
        EMBED_DIM = 256
        NUM_HEAD = 16
        NEG_BIG = 10000000000.0
        B, S, E = x.shape
        H = NUM_HEAD
        y = jnp.einsum('bse,ef->bsf', x, W1) + b1
        y = y.reshape(B, S, H, -1).transpose(0, 2, 1, 3)
        q, k, v = jnp.split(y, 3, axis=-1)
        dk = jnp.asarray(v.shape[-1], x.dtype) ** 0.5
        w = jnp.einsum('bhqd,bhkd->bhqk', q, k) / dk
        mask = jnp.tril(jnp.ones((S, S), dtype=x.dtype))
        w = w * mask - NEG_BIG * (1.0 - mask)
        w = jax.nn.softmax(w, axis=-1)
        attn = jnp.einsum('bhqk,bhkd->bhqd', w, v)
        attn = attn.transpose(0, 2, 1, 3).reshape(B, S, E)
        return jnp.einsum('bse,ef->bsf', attn, W2) + b2

    def _L0_ffn_ref(x, gate_w, expert_bias, w_gate, w_up, w_down, shared_gate_w, shared_up_w, shared_down_w):
        import jax, jax.numpy as jnp
        import numpy as np
        B, S, D = (2, 128, 256)
        E, K, I = (16, 8, 256)
        I_SH = 256
        ROUTE_SCALE = 2.826
        gates = jnp.einsum('bsd,ed->bse', x, gate_w)
        scores = jax.nn.sigmoid(gates.astype(jnp.float32))
        sel_scores = scores + expert_bias
        _, inds = jax.lax.top_k(sel_scores, K)
        selected = jnp.take_along_axis(scores, inds, axis=-1)
        selected = selected / selected.sum(axis=-1, keepdims=True)
        selected = selected * ROUTE_SCALE
        onehot = jax.nn.one_hot(inds, E, dtype=selected.dtype)
        combine = jnp.einsum('bske,bsk->bse', onehot, selected)
        hg = jnp.einsum('bsd,eid->bsei', x, w_gate)
        hu = jnp.einsum('bsd,eid->bsei', x, w_up)
        h = jax.nn.silu(hg) * hu
        ye = jnp.einsum('bsei,edi->bsed', h, w_down)
        y = jnp.einsum('bsed,bse->bsd', ye, combine).astype(x.dtype)
        g = jnp.einsum('bsd,id->bsi', x, shared_gate_w)
        u = jnp.einsum('bsd,id->bsi', x, shared_up_w)
        y = y + jnp.einsum('bsi,di->bsd', jax.nn.silu(g) * u, shared_down_w)
        return y
    x = L0_attn_x
    x = x + _layernorm(_L0_attn_ref(_layernorm(x, axis=-1), L0_attn_W1, L0_attn_b1, L0_attn_W2, L0_attn_b2), axis=-1)
    x = x + _layernorm(_L0_ffn_ref(_layernorm(x, axis=-1), L0_ffn_gate_w, L0_ffn_expert_bias, L0_ffn_w_gate, L0_ffn_w_up, L0_ffn_w_down, L0_ffn_shared_gate_w, L0_ffn_shared_up_w, L0_ffn_shared_down_w), axis=-1)
    return x

_drawn_inputs = setup_inputs


def setup_inputs(seed=0):
    import zlib

    import numpy as np

    out = dict(_drawn_inputs(seed))
    spreads = {'L0_ffn_expert_bias': (0.0, 0.1)}
    factors = {}
    for name, (base, spread) in spreads.items():
        noise = np.random.default_rng([zlib.crc32(name.encode()), seed]).standard_normal(out[name].shape)
        drawn = base * np.exp(spread * noise) if base else spread * noise
        out[name] = jnp.asarray(drawn.astype(out[name].dtype))
    for name, factor in factors.items():
        out[name] = (out[name] * factor).astype(out[name].dtype)
    return out
```

```python
from contextlib import ExitStack

import numpy as np

import concourse.bass as bass
from concourse import mybir

ALU = mybir.AluOpType
ACT = mybir.ActivationFunctionType
AX = mybir.AxisListType
F32 = mybir.dt.float32
F32R = mybir.dt.float32r
BF16 = mybir.dt.bfloat16

P = 128
EPS = 1e-5
B, S, D, H, DH = 8, 1024, 256, 16, 16
T = B * S
TILE = 512
NT = T // TILE
SUB = TILE // P
KC = D // P
HG = 4
NGH = H // HG
NG = B * NGH
SLOT = 32
NBLK = S // P
NE, TOPK, F = 16, 8, 256
ROUTE_SCALE = 2.826
MASK = -4e10
GT = 4
BASE = 1
NGR = NT // GT


class Mem:

    def __init__(self, nc, outer, inner, stage):
        self.nc, self.outer, self.inner, self.stage = nc, outer, inner, stage
        self.sems = []

    def sb(self, name, shape, dt=F32):
        return self.inner.enter_context(self.nc.sbuf_tensor(f"{self.stage}_{name}", shape, dt))

    def ps(self, name, shape, dt=F32):
        return self.inner.enter_context(self.nc.psum_tensor(f"{self.stage}_{name}", shape, dt))

    def sem(self, name, lifted=True):
        s = self.outer.enter_context(self.nc.semaphore(f"{self.stage}_{name}"))
        if lifted:
            self.sems.append(s)
        return s

    def lift(self, eng):
        for s in self.sems:
            eng.sem_inc(s, BASE)


def three_products(pe, out, lhs_hi, lhs_lo, rhs_hi, rhs_lo, chunks):
    pairs = [(lhs_hi, rhs_hi), (lhs_hi, rhs_lo), (lhs_lo, rhs_hi)]
    last = None
    for c in range(chunks):
        for n, (a, b) in enumerate(pairs):
            last = pe.matmul(out, a(c), b(c), start=(c == 0 and n == 0), stop=(c == chunks - 1 and n == 2))
    return last


class Norm:

    def __init__(self, m, name):
        self.spare = m.sb(f"{name}_spare", [P, 1])
        self.const = m.sb(f"{name}_const", [P, 2])
        self.st = m.sb(f"{name}_stats", [P, SUB, 6])
        self.mv = m.sb(f"{name}_meanvar", [P, SUB, 2])
        self.ve = m.sb(f"{name}_var_eps", [P, SUB])
        self.rs = m.sb(f"{name}_rstd", [P, SUB])
        self.set, self.stats, self.aggr, self.added, self.power, self.done = (
            m.sem(f"{name}_{k}") for k in ("set", "stats", "aggr", "added", "power", "done"))

    def constants(self, pool):
        pool.memset(self.const[:, 0:1], EPS).then_inc(self.set, 1)
        pool.memset(self.const[:, 1:2], -0.5).then_inc(self.set, 1)
        pool.wait_ge(self.set, BASE + 2)

    def root(self, pool, t):
        pool.wait_ge(self.aggr, BASE + t + 1)
        pool.tensor_tensor(self.ve[:], self.mv[:, :, 1], self.const[:, 0:1].broadcast_to((P, SUB)), ALU.add
                           ).then_inc(self.added, 1)
        pool.wait_ge(self.added, BASE + t + 1)
        pool.wait_ge(self.done, BASE + t)
        pool.tensor_tensor(self.rs[:], self.ve[:], self.const[:, 1:2].broadcast_to((P, SUB)), ALU.pow
                           ).then_inc(self.power, 1)

    def moments(self, dve, t, src):
        for s in range(SUB):
            last = dve.bn_stats(self.st[:, s], src(s))
        last.then_inc(self.stats, 1)
        dve.wait_ge(self.stats, BASE + t + 1)
        dve.memset(self.spare[:], 0.0)
        for s in range(SUB):
            last = dve.bn_aggr(self.mv[:, s], self.st[:, s])
        last.then_inc(self.aggr, 1)

    def apply(self, dve, t, src, dst):
        dve.wait_ge(self.power, BASE + t + 1)
        for s in range(SUB):
            last = dve.tensor_scalar(dst(s), src(s), self.mv[:, s, 0:1], self.rs[:, s:s + 1],
                                     ALU.subtract, ALU.mult)
        last.then_inc(self.done, 1)


def pipelined(eng, step):
    with eng.Fori(0, NT // 2 - 1) as it:
        for r in range(2):
            step(it * 2 + r, r, True)
    step(NT - 2, 0, True)
    step(NT - 1, 1, False)


def project_qkv(nc, outer, x, w1, b1c, b1v, ident_in, qk_dram, v_dram):
    with ExitStack() as inner:
        m = Mem(nc, outer, inner, "A")
        xt = m.sb("x", [P, 2, SUB, D])
        xn = m.sb("xn", [P, SUB, D])
        ident = m.sb("ident", [P, P])
        ws = m.sb("w_stage", [P, KC, 3 * D])
        wh = m.sb("w_hi", [P, KC, 3 * D], F32R)
        wl = m.sb("w_lo", [P, KC, 3 * D], F32R)
        bc = m.sb("bias_qk", [P, 4])
        bv = m.sb("bias_v", [P, D])
        xh = m.sb("xT_hi", [P, 2, KC, TILE], F32R)
        xl = m.sb("xT_lo", [P, 2, KC, TILE], F32R)
        qh = m.sb("qk_hi", [P, 2, 4, TILE], F32R)
        ql = m.sb("qk_lo", [P, 2, 4, TILE], F32R)
        vt = m.sb("v", [P, 2, SUB, H, SLOT])
        ps_x = m.ps("ps_xT", [P, KC, TILE])
        ps_q = m.ps("ps_qk", [P, 4, TILE])
        ps_v = m.ps("ps_v", [P, 2, 2, D])

        s_w, s_ones, s_wh, s_wsplit = m.sem("weights_loaded"), m.sem("ones"), m.sem("w_hi"), m.sem("w_split")
        s_x = [m.sem(f"x_loaded{i}") for i in range(2)]
        norm = Norm(m, "norm")
        s_xT, s_xh, s_xl = m.sem("transposed"), m.sem("xT_hi_done"), m.sem("xT_split")
        s_q, s_qh, s_ql = m.sem("qk_product"), m.sem("qk_hi_done"), m.sem("qk_split")
        s_v, s_vc = m.sem("v_product"), m.sem("v_copied")
        s_st = [m.sem(f"stored{i}") for i in range(2)]
        STORES = 4 * 2 + SUB

        with nc.Block() as block:

            @block.sync
            def _(sp):
                sp.dma_start(xt[:, 0], x[0:TILE, :].rearrange("(s p) d -> p s d", p=P)).then_inc(s_x[0], 16)
                sp.dma_start(ident[:], ident_in).then_inc(s_w, 16)
                sp.dma_start(ws[:], w1.rearrange("(c p) f -> p c f", p=P)).then_inc(s_w, 16)
                sp.dma_start(bc[:], b1c).then_inc(s_w, 16)
                sp.dma_start(bv[:], b1v).then_inc(s_w, 16)
                sp.dma_start(xt[:, 1], x[TILE:2 * TILE, :].rearrange("(s p) d -> p s d", p=P)).then_inc(s_x[1], 16)

                def step(t, r, more):
                    if more:
                        sp.wait_ge(norm.done, BASE + t + 1)
                        sp.dma_start(xt[:, r], x[bass.ds((t + 2) * TILE, TILE), :].rearrange(
                            "(s p) d -> p s d", p=P)).then_inc(s_x[r], 16)
                    b_, half = t // 2, r
                    for c in range(4):
                        sp.wait_ge(s_ql, BASE + 4 * t + c + 1)
                        for hl, src in enumerate((qh, ql)):
                            sp.dma_start(qk_dram[c // 2, hl, bass.ds(b_ * D + (c % 2) * P, P),
                                                 half * TILE:(half + 1) * TILE], src[:, r, c].bitcast(F32)).then_inc(s_st[r], 16)
                    sp.wait_ge(s_vc, BASE + 2 * t + 2)
                    for s in range(SUB):
                        sp.dma_start(v_dram[bass.ds(b_ * NGH, NGH), half * SUB + s].rearrange("g p f -> p g f"),
                                     vt[:, r, s].rearrange("p (g h) e -> p g (h e)", g=NGH)).then_inc(s_st[r], 16)

                with sp.Fori(0, NT // 2 - 1) as it:
                    for r in range(2):
                        step(it * 2 + r, r, True)
                step(NT - 2, 0, False)
                step(NT - 1, 1, False)
                for r in range(2):
                    sp.wait_ge(s_st[r], BASE + 16 * STORES * NT // 2)

            @block.gpsimd
            def _(pool):
                m.lift(pool)
                norm.constants(pool)
                norm.root(pool, 0)
                pipelined(pool, lambda t, r, more: norm.root(pool, t + 1) if more else None)

            @block.vector
            def _(dve):
                dve.wait_ge(s_w, BASE + 64)
                dve.wait_ge(s_wh, BASE + 1)
                dve.tensor_tensor(wl[:], ws[:], wh[:].bitcast(F32), ALU.subtract).then_inc(s_wsplit, 1)

                def front(t, r):
                    dve.wait_ge(s_x[r], BASE + (t // 2 + 1) * 16)
                    norm.moments(dve, t, lambda s: xt[:, r, s])
                    dve.wait_ge(s_xT, BASE + t)
                    norm.apply(dve, t, lambda s: xt[:, r, s], lambda s: xn[:, s])

                def split(t, r):
                    dve.wait_ge(s_xh, BASE + t + 1)
                    dve.tensor_tensor(xl[:, r], ps_x[:], xh[:, r].bitcast(F32), ALU.subtract).then_inc(s_xl, 1)

                def step(t, r, more):
                    if more:
                        front(t + 1, 1 - r)
                    for c in range(4):
                        dve.wait_ge(s_qh, BASE + 4 * t + c + 1)
                        dve.scalar_tensor_tensor(ql[:, r, c], ps_q[:, c], bc[:, c:c + 1], qh[:, r, c].bitcast(F32),
                                                 ALU.add, ALU.subtract).then_inc(s_ql, 1)
                    if more:
                        split(t + 1, 1 - r)
                    dve.wait_ge(s_st[r], BASE + (t // 2) * 16 * STORES)
                    for k in range(2):
                        dve.wait_ge(s_v, BASE + 2 * t + k + 1)
                        for j in range(2):
                            s = 2 * k + j
                            last = dve.tensor_tensor(vt[:, r, s, :, 0:DH],
                                                     ps_v[:, k, j].rearrange("p (h e) -> p h e", h=H),
                                                     bv[:].rearrange("p (h e) -> p h e", h=H), ALU.add)
                        last.then_inc(s_vc, 1)

                dve.memset(vt[:, :, :, :, DH:SLOT], 1.0).then_inc(s_ones, 1)
                front(0, 0)
                split(0, 0)
                pipelined(dve, step)

            @block.scalar
            def _(act):
                act.wait_ge(s_w, BASE + 64)
                act.activation(wh[:], ws[:], ACT.Copy).then_inc(s_wh, 1)

                def split(t, r):
                    act.wait_ge(s_xT, BASE + t + 1)
                    act.activation(xh[:, r], ps_x[:], ACT.Copy).then_inc(s_xh, 1)

                def step(t, r, more):
                    act.wait_ge(s_st[r], BASE + (t // 2) * 16 * STORES)
                    for c in range(4):
                        act.wait_ge(s_q, BASE + 4 * t + c + 1)
                        act.activation(qh[:, r, c], ps_q[:, c], ACT.Identity, bias=bc[:, c:c + 1]).then_inc(s_qh, 1)
                    if more:
                        split(t + 1, 1 - r)

                split(0, 0)
                pipelined(act, step)

            @block.tensor
            def _(pe):
                pe.wait_ge(s_w, BASE + 64)

                def transposes(t):
                    pe.wait_ge(norm.done, BASE + t + 1)
                    pe.wait_ge(s_xl, BASE + t)
                    for c in range(KC):
                        for s in range(SUB):
                            last = pe.transpose(ps_x[:, c, s * P:(s + 1) * P], xn[:, s, c * P:(c + 1) * P], ident[:])
                    last.then_inc(s_xT, 1)

                def step(t, r, more):
                    pe.wait_ge(s_xl, BASE + t + 1)
                    for c in range(4):
                        pe.wait_ge(s_ql, BASE + 4 * t)
                        three_products(pe, ps_q[:, c], lambda k: wh[:, k, c * P:(c + 1) * P],
                                       lambda k: wl[:, k, c * P:(c + 1) * P], lambda k: xh[:, r, k],
                                       lambda k: xl[:, r, k], KC).then_inc(s_q, 1)
                    if more:
                        transposes(t + 1)
                    for k2 in range(2):
                        pe.wait_ge(s_vc, BASE + 2 * t)
                        for j in range(2):
                            s = 2 * k2 + j
                            last = three_products(pe, ps_v[:, k2, j], lambda k: xh[:, r, k, s * P:(s + 1) * P],
                                                  lambda k: xl[:, r, k, s * P:(s + 1) * P],
                                                  lambda k: wh[:, k, 2 * D:3 * D], lambda k: wl[:, k, 2 * D:3 * D], KC)
                        last.then_inc(s_v, 1)

                transposes(0)
                pe.wait_ge(s_wsplit, BASE + 1)
                pipelined(pe, step)


UNITS = [(i, (h, h + 1)) for i in range(4) for h in (0, 2)] + [(i, (h,)) for i in range(4, NBLK) for h in range(HG)]
FIRST = len(UNITS)
KEYS = [(qh, j) for qh in range(2) for j in range(4 * (qh + 1))]
QUADS = len(KEYS)
SLOTS = 3
STACK = 3 * DH
PAD = 96
SHIFT = PAD + 2
HALF = KEYS.index((1, 0))


def width(qh, j):
    return TILE - max(0, j * P - qh * TILE)


def schedule():
    units, first = [], 0
    for k in range(2 * QUADS):
        units.append(("second", 2 + k))
        for _ in range(2 if k % 3 == 0 else 1):
            if first < FIRST:
                units.append(("first", first))
                first += 1
    return units


def attention(nc, outer, ident_in, identb_in, mask_in, maskT_in, qk_dram, v_dram, a_dram, den_dram):
    with ExitStack() as inner:
        m = Mem(nc, outer, inner, "B")
        qs = m.sb("q_stack", [P, 3, HG, S], F32R)
        ks = m.sb("k_stack", [P, 3, HG, S], F32R)
        vs = m.sb("v", [P, 3, NBLK, HG * SLOT])
        pt = m.sb("probs", [P, SLOTS, HG, TILE])
        mx = m.sb("max", [P, HG, NBLK])
        mh = m.sb("neg_max_hi", [HG * NBLK, P], F32R)
        ml = m.sb("neg_max_lo", [HG * NBLK, P], F32R)
        ident = m.sb("ident", [P, P])
        identb = m.sb("ident_bf", [P, P], BF16)
        mask = m.sb("mask", [P, P], BF16)
        maskT = m.sb("maskT", [P, P], BF16)
        on = m.sb("out_raw", [P, 2, TILE])
        stage = m.sb("mask_stage", [P, 3, P])
        ps = m.ps("slots", [P, SLOTS, 2 * TILE])
        po = m.ps("ps_out", [P, TILE])
        pm = m.ps("ps_maxT", [P, TILE])

        s_c, s_set, s_kset = m.sem("constants_loaded"), m.sem("constants_set"), m.sem("k_constants_set")
        s_ld = [m.sem(f"group_loaded{i}") for i in range(3)]
        s_sc1, s_max = m.sem("first_scores"), m.sem("first_max")
        s_mT, s_mh, s_ml, s_row = m.sem("maxT"), m.sem("neg_max_hi"), m.sem("neg_max"), m.sem("max_rows")
        s_sc2, s_exp = m.sem("second_scores"), m.sem("exped")
        s_pfree = m.sem("probs_free")
        s_on = m.sem("out_raw")
        s_st = [m.sem(f"out_stored{i}") for i in range(2)]
        LOADS, STORES = 7, 16 * 2 * HG
        sched = schedule()

        def in_loop(eng, step):
            with eng.Fori(0, NG // 3) as it:
                for r in range(3):
                    step(it * 3 + r, r, True)
            step(NG - 2, 0, True)
            step(NG - 1, 1, False)

        with nc.Block() as block:

            @block.sync
            def _(sp):
                def load(g, r):
                    for row, hl in ((0, 0), (1, 1), (2, 0)):
                        sp.dma_start(qs[row * DH:(row + 1) * DH, r].bitcast(F32), qk_dram[
                            0, hl, bass.ds(g * HG * DH, HG * DH), :].rearrange("(h d) n -> d h n", d=DH)
                        ).then_inc(s_ld[r], 16)
                    for row, hl in ((0, 0), (1, 0), (2, 1)):
                        sp.dma_start(ks[row * DH:(row + 1) * DH, r].bitcast(F32), qk_dram[
                            1, hl, bass.ds(g * HG * DH, HG * DH), :].rearrange("(h d) n -> d h n", d=DH)
                        ).then_inc(s_ld[r], 16)
                    sp.dma_start(vs[:, r], v_dram[bass.ds(g, 1)].rearrange("o j p f -> p (o j) f")
                                 ).then_inc(s_ld[r], 16)

                def max_rows(g, r):
                    sp.wait_ge(s_ml, BASE + g + 1)
                    for row, src in ((PAD, mh), (PAD + 1, ml)):
                        sp.dma_start(qs[row:row + 1, r].bitcast(F32).rearrange("o h (i q) -> o (h i) q", q=P),
                                     src[:].bitcast(F32)).then_inc(s_row, 16)

                def store(g, qh):
                    sp.wait_ge(s_on, BASE + 2 * g + qh + 1)
                    for h in range(HG):
                        sp.dma_start(a_dram[bass.ds(g * HG * DH + h * DH, DH), qh * TILE:(qh + 1) * TILE],
                                     on[h * SLOT:h * SLOT + DH, qh]).then_inc(s_st[qh], 16)
                        sp.dma_start(den_dram[bass.ds(g * HG + h, 1), qh * TILE:(qh + 1) * TILE],
                                     on[h * SLOT + DH:h * SLOT + DH + 1, qh]).then_inc(s_st[qh], 16)

                sp.dma_start(ident[:], ident_in).then_inc(s_c, 16)
                sp.dma_start(stage[:, 0], identb_in).then_inc(s_c, 16)
                sp.dma_start(stage[:, 1], mask_in).then_inc(s_c, 16)
                sp.dma_start(stage[:, 2], maskT_in).then_inc(s_c, 16)
                sp.wait_ge(s_set, BASE + 1)
                sp.wait_ge(s_kset, BASE + 2)
                for r in range(3):
                    load(r, r)
                max_rows(0, 0)

                def step(g, r, more, loads):
                    if more:
                        max_rows(g + 1, (r + 1) % 3)
                    store(g, 0)
                    if loads:
                        sp.wait_ge(s_pfree, BASE + SLOTS + (g + 1) * QUADS)
                        load(g + 3, r)
                    store(g, 1)

                with sp.Fori(0, NG // 3 - 1) as it:
                    for r in range(3):
                        step(it * 3 + r, r, True, True)
                for g in range(NG // 3 * 3 - 3, NG):
                    step(g, g % 3, g + 1 < NG, g + 3 < NG)
                for qh in range(2):
                    sp.wait_ge(s_st[qh], BASE + NG * STORES)

            @block.gpsimd
            def _(pool):
                m.lift(pool)
                pool.memset(ks[0:PAD].bitcast(F32), 0.0).then_inc(s_kset, 1)
                pool.memset(ks[PAD:P].bitcast(F32), 1.0).then_inc(s_kset, 1)

            @block.vector
            def _(dve):
                dve.memset(qs[:].bitcast(F32), 0.0).then_inc(s_set, 1)
                dve.wait_ge(s_c, BASE + 64)
                dve.tensor_copy(identb[:], stage[:, 0]).then_inc(s_set, 1)
                dve.tensor_copy(mask[:], stage[:, 1]).then_inc(s_set, 1)
                dve.tensor_copy(maskT[:], stage[:, 2]).then_inc(s_set, 1)

                def maxima(g, u, slot):
                    i, heads = UNITS[u]
                    w = (i + 1) * P
                    dve.wait_ge(s_sc1, BASE + g * FIRST + u + 1)
                    if u == 0:
                        dve.wait_ge(s_mT, BASE + g)
                    if len(heads) == 2:
                        src = ps[:, slot].rearrange("p (h n) -> p h n", h=2)[:, :, 0:w]
                    else:
                        src = ps[:, slot, 0:w]
                    dve.tensor_reduce(mx[:, heads[0]:heads[-1] + 1, i], src, AX.X, ALU.max).then_inc(s_max, 1)

                def rows(g):
                    dve.wait_ge(s_mT, BASE + g + 1)
                    dve.wait_ge(s_row, BASE + 32 * g)
                    n = HG * NBLK
                    dve.tensor_scalar(mh[:], pm[0:n, 0:P], -1.0, None, ALU.mult).then_inc(s_mh, 1)
                    dve.wait_ge(s_mh, BASE + g + 1)
                    dve.scalar_tensor_tensor(ml[:], pm[0:n, 0:P], -1.0, mh[:].bitcast(F32), ALU.mult,
                                             ALU.subtract).then_inc(s_ml, 1)

                for u in range(FIRST):
                    maxima(0, u, u % SLOTS)
                rows(0)

                def step(g, r, more):
                    for n, (kind, u) in enumerate(sched):
                        if kind == "first" and more:
                            maxima(g + 1, u, n % SLOTS)
                    if more:
                        rows(g + 1)

                in_loop(dve, step)

            @block.scalar
            def _(act):
                def exps(g, v, slot):
                    qh, j = KEYS[v // 2 % QUADS]
                    buf = v // 2 % SLOTS
                    w = width(qh, j)
                    act.wait_ge(s_sc2, BASE + g * 2 * QUADS + v + 1)
                    if v % 2 == 0:
                        act.wait_ge(s_pfree, BASE + g * QUADS + v // 2 + 1)
                    h = v % 2 * 2
                    act.activation(pt[:, buf, h:h + 2, 0:w], ps[:, slot].rearrange("p (h n) -> p h n", h=2)[:, :, 0:w],
                                   ACT.Exp, scale=float(DH) ** -0.5).then_inc(s_exp, 1)

                def raw(g, qh):
                    act.wait_ge(s_pfree, BASE + SLOTS + g * QUADS + (QUADS if qh else HALF))
                    act.wait_ge(s_st[qh], BASE + g * STORES)
                    act.activation(on[:, qh], po[:], ACT.Copy).then_inc(s_on, 1)

                for v in range(2):
                    exps(0, v, 1 + v)

                def step(g, r, more):
                    for n, (kind, v) in enumerate(sched):
                        if kind == "second" and (more or v < 2 * QUADS):
                            exps(g, v, n % SLOTS)
                        if (kind, v) == ("second", 2 * HALF + 2):
                            raw(g, 0)
                    raw(g, 1)

                in_loop(act, step)

            @block.tensor
            def _(pe):
                pe.sem_inc(s_pfree, SLOTS)
                pe.wait_ge(s_set, BASE + 4)

                def first(g, r, u, slot):
                    i, heads = UNITS[u]
                    w = (i + 1) * P
                    for b, h in enumerate(heads):
                        o = ps[:, slot, b * TILE:(b + 1) * TILE]
                        q = qs[0:PAD, r, h, i * P:(i + 1) * P]
                        if w > TILE:
                            pe.matmul(o, q, ks[0:PAD, r, h, 0:TILE], start=True, stop=True)
                            o = ps[:, slot, TILE:2 * TILE]
                            pe.matmul(o[:, 0:w - TILE], q, ks[0:PAD, r, h, TILE:w], start=True, stop=False)
                        else:
                            pe.matmul(o[:, 0:w], q, ks[0:PAD, r, h, 0:w], start=True, stop=False)
                        at = (w - P) % TILE
                        last = pe.matmul(o[:, at:at + P], identb[:], mask[:], start=False, stop=True)
                    last.then_inc(s_sc1, 1)

                def second(g, r, v, slot):
                    qh, j = KEYS[v // 2 % QUADS]
                    w = width(qh, j)
                    q0 = (qh + 1) * TILE - w
                    for b in range(2):
                        h = v % 2 * 2 + b
                        o = ps[:, slot, b * TILE:b * TILE + w]
                        diagonal = q0 == j * P
                        last = pe.matmul(o, ks[0:SHIFT, r, h, j * P:(j + 1) * P], qs[0:SHIFT, r, h, q0:q0 + w],
                                         start=True, stop=not diagonal)
                        if diagonal:
                            last = pe.matmul(o[:, 0:P], identb[:], maskT[:], start=False, stop=True)
                    last.then_inc(s_sc2, 1)

                def values(g, r, k):
                    qh, j = KEYS[k]
                    w = width(qh, j)
                    pe.wait_ge(s_exp, BASE + g * 2 * QUADS + 2 * k + 2)
                    if j == 0:
                        pe.wait_ge(s_on, BASE + 2 * g + qh)
                    for h in range(HG):
                        last = pe.matmul(po[h * SLOT:(h + 1) * SLOT, TILE - w:TILE], vs[:, r, j, h * SLOT:(h + 1) * SLOT],
                                         pt[:, k % SLOTS, h, 0:w], start=(j == 0), stop=(j == 4 * (qh + 1) - 1))
                    last.then_inc(s_pfree, 1)

                def max_transpose(g):
                    pe.wait_ge(s_max, BASE + (g + 1) * FIRST)
                    pe.wait_ge(s_ml, BASE + g)
                    pe.transpose(pm[0:HG * NBLK, 0:P], mx[:].rearrange("p h i -> p (h i)"), ident[:]).then_inc(s_mT, 1)

                def group_loaded(g, r):
                    pe.wait_ge(s_ld[r], BASE + (g // 3 + 1) * 16 * LOADS)

                group_loaded(0, 0)
                for u in range(FIRST):
                    if u >= SLOTS:
                        pe.wait_ge(s_max, BASE + u - SLOTS + 1)
                    first(0, 0, u, u % SLOTS)
                max_transpose(0)
                pe.wait_ge(s_row, BASE + 32)
                for v in range(2):
                    second(0, 0, v, 1 + v)

                def slot_free(g, n, more):
                    p = n - SLOTS
                    if p < 0:
                        pe.wait_ge(s_exp, BASE + g * 2 * QUADS + p + SLOTS)
                        return
                    kind, u = sched[p]
                    if kind == "first":
                        if more:
                            pe.wait_ge(s_max, BASE + (g + 1) * FIRST + u + 1)
                    else:
                        pe.wait_ge(s_exp, BASE + g * 2 * QUADS + u + 1)

                def step(g, r, more):
                    if more:
                        group_loaded(g + 1, (r + 1) % 3)
                    for n, (kind, u) in enumerate(sched):
                        if kind == "first":
                            if more:
                                slot_free(g, n, more)
                                first(g + 1, (r + 1) % 3, u, n % SLOTS)
                            continue
                        if u < 2 * QUADS:
                            slot_free(g, n, more)
                            second(g, r, u, n % SLOTS)
                        elif more:
                            slot_free(g, n, more)
                            if u == 2 * QUADS:
                                pe.wait_ge(s_row, BASE + 32 * (g + 2))
                            second(g + 1, (r + 1) % 3, u - 2 * QUADS, n % SLOTS)
                        if u % 2 == 1:
                            values(g, r, u // 2 - 1)
                        if more and u == 2 * QUADS - 3:
                            max_transpose(g + 1)

                in_loop(pe, step)


def output_and_route(nc, outer, x, w2, b2, gate, ebias, ident_in, a_dram, den_dram, inv_dram,
                     x1_dram, xT_dram, combine):
    with ExitStack() as inner:
        m = Mem(nc, outer, inner, "C")
        at = m.sb("attnT", [P, 2, KC, TILE])
        den = m.sb("denominators", [P, S])
        ib = m.sb("inverse_rows", [P, 2, KC, TILE])
        an = m.sb("attnT_normed", [P, KC, TILE])
        ah = m.sb("attnT_hi", [P, KC, TILE], F32R)
        al = m.sb("attnT_lo", [P, KC, TILE], F32R)
        xt = m.sb("x", [P, 2, SUB, D])
        zb = m.sb("z", [P, SUB, D])
        zn = m.sb("z_normed", [P, SUB, D])
        x1 = m.sb("x1", [P, 2, SUB, D])
        xn = m.sb("x1_normed", [P, SUB, D])
        xh = m.sb("xT_hi", [P, 2, KC, TILE], F32R)
        xl = m.sb("xT_lo", [P, 2, KC, TILE], F32R)
        ws = m.sb("w_stage", [P, KC, D + NE])
        wh = m.sb("w_hi", [P, KC, D + NE], F32R)
        wl = m.sb("w_lo", [P, KC, D + NE], F32R)
        bb = m.sb("bias_out", [P, D])
        eb = m.sb("bias_expert", [P, NE])
        ident = m.sb("ident", [P, P])
        spare = m.sb("spare", [P, 1])
        th = m.sb("tanh", [P, SUB, NE])
        sc = m.sb("scores", [P, SUB, NE])
        sel = m.sb("scores_biased", [P, SUB, NE])
        top = m.sb("top8", [P, SUB, TOPK])
        rest = m.sb("rest", [P, SUB, NE])
        pick = m.sb("picked", [P, SUB, NE])
        part = m.sb("picked_scores", [P, SUB, NE])
        tot = m.sb("picked_sum", [P, SUB])
        inv = m.sb("picked_inverse", [P, SUB])
        ps_z = m.ps("ps_z", [P, SUB, D])
        ps_x = m.ps("ps_xT", [P, KC, TILE])
        ps_r = m.ps("ps_router", [P, SUB, NE])

        s_w, s_wh, s_wl = (m.sem(n) for n in ("weights_loaded", "w_hi", "w_split"))
        s_den, s_inv, s_invs = (m.sem(n) for n in ("den_loaded", "inverses", "inverses_stored"))
        LOADS = 16 * (2 + H)
        z_norm, x_norm = Norm(m, "norm_z"), Norm(m, "norm_x1")
        s_ld = [m.sem(f"tile_loaded{i}") for i in range(2)]
        s_an = m.sem("attnT_normed")
        s_ah, s_al, s_z, s_zb, s_x1 = (m.sem(n) for n in ("attnT_hi", "attnT_split", "z", "z_biased", "x1_done"))
        s_xT, s_xh, s_xl, s_r = (m.sem(n) for n in ("transposed", "xT_hi", "xT_split", "router_product"))
        s_th, s_sc, s_sel, s_top, s_rest, s_pick, s_part, s_tot, s_ti, s_c = (m.sem(n) for n in (
            "tanh", "scores", "biased", "top8", "rest", "picked", "picked_scores", "picked_sum", "sum_inverse", "combine"))
        s_st = [m.sem(f"stored{i}") for i in range(2)]

        with nc.Block() as block:

            @block.sync
            def _(sp):
                def load(b_, r):
                    sp.dma_start(at[:, r], a_dram[bass.ds(b_ * D, D), r * TILE:(r + 1) * TILE].rearrange(
                        "(c p) n -> p c n", p=P)).then_inc(s_ld[r], 16)
                    sp.dma_start(xt[:, r], x[bass.ds(b_ * S + r * TILE, TILE), :].rearrange(
                        "(s p) d -> p s d", p=P)).then_inc(s_ld[r], 16)
                    for c in range(KC):
                        for k in range(P // DH):
                            sp.dma_start(ib[k * DH:(k + 1) * DH, r, c], inv_dram[
                                bass.ds(b_ * H + c * (P // DH) + k, 1), r * TILE:(r + 1) * TILE].broadcast_to(
                                    (DH, TILE))).then_inc(s_ld[r], 16)

                def store(t, r):
                    sp.wait_ge(s_x1, BASE + t + 1)
                    sp.dma_start(x1_dram[bass.ds(t, 1)].rearrange("o p s d -> p (o s) d"), x1[:, r]).then_inc(s_st[r], 16)
                    sp.wait_ge(s_xl, BASE + t + 1)
                    for hl, src in enumerate((xh, xl)):
                        sp.dma_start(xT_dram[bass.ds(t, 1), hl].rearrange("o p c n -> p (o c) n"),
                                     src[:, r].bitcast(F32)).then_inc(s_st[r], 16)

                sp.dma_start(den[:], den_dram).then_inc(s_den, 16)
                sp.dma_start(ws[:, :, 0:D], w2.rearrange("(c p) f -> p c f", p=P)).then_inc(s_w, 16)
                sp.dma_start(ws[:, :, D:D + NE], gate.rearrange("(c p) f -> p c f", p=P)).then_inc(s_w, 16)
                sp.dma_start(bb[:], b2).then_inc(s_w, 16)
                sp.dma_start(eb[:], ebias).then_inc(s_w, 16)
                sp.dma_start(ident[:], ident_in).then_inc(s_w, 16)
                sp.wait_ge(s_inv, BASE + 1)
                sp.dma_start(inv_dram, den[:]).then_inc(s_invs, 16)
                sp.wait_ge(s_invs, BASE + 16)
                load(0, 0)
                load(0, 1)

                def step(b_, r, more):
                    t = b_ * 2 + r
                    if more:
                        sp.wait_ge(s_x1, BASE + t + 1)
                        load(b_ + 1, r)
                    store(t, r)

                with sp.Fori(0, B - 1) as b_:
                    for r in range(2):
                        step(b_, r, True)
                for r in range(2):
                    step(B - 1, r, False)
                for r in range(2):
                    sp.wait_ge(s_st[r], BASE + 48 * NT // 2)

            @block.gpsimd
            def _(pool):
                m.lift(pool)

                def residual(t, r):
                    pool.wait_ge(s_ld[r], BASE + LOADS * (t // 2 + 1))
                    pool.wait_ge(z_norm.done, BASE + t + 1)
                    pool.wait_ge(s_st[r], BASE + 48 * (t // 2))
                    pool.tensor_tensor(x1[:, r], xt[:, r], zn[:], ALU.add).then_inc(s_x1, 1)

                def step(t, r, more):
                    x_norm.root(pool, t)
                    if more:
                        z_norm.root(pool, t + 1)
                        residual(t + 1, 1 - r)

                z_norm.constants(pool)
                x_norm.constants(pool)
                z_norm.root(pool, 0)
                residual(0, 0)
                pipelined(pool, step)

            @block.vector
            def _(dve):
                dve.wait_ge(s_den, BASE + 16)
                dve.reciprocal(den[:], den[:]).then_inc(s_inv, 1)
                dve.wait_ge(s_w, BASE + 80)
                dve.wait_ge(s_wh, BASE + 1)
                dve.tensor_tensor(wl[:], ws[:], wh[:].bitcast(F32), ALU.subtract).then_inc(s_wl, 1)

                def split_attn(t, r):
                    dve.wait_ge(s_ld[r], BASE + LOADS * (t // 2 + 1))
                    dve.tensor_tensor(an[:], at[:, r], ib[:, r], ALU.mult).then_inc(s_an, 1)
                    dve.wait_ge(s_ah, BASE + t + 1)
                    dve.tensor_tensor(al[:], an[:], ah[:].bitcast(F32), ALU.subtract).then_inc(s_al, 1)

                def bias_and_norm(t, r):
                    for k in range(2):
                        dve.wait_ge(s_z, BASE + 2 * t + k + 1)
                        for s in range(2 * k, 2 * k + 2):
                            last = dve.tensor_tensor(zb[:, s], ps_z[:, s], bb[:], ALU.add)
                        last.then_inc(s_zb, 1)
                    dve.wait_ge(s_zb, BASE + 2 * t + 2)
                    z_norm.moments(dve, t, lambda s: zb[:, s])
                    dve.wait_ge(s_x1, BASE + t)
                    z_norm.apply(dve, t, lambda s: zb[:, s], lambda s: zn[:, s])

                def norm_x1(t, r):
                    dve.wait_ge(s_x1, BASE + t + 1)
                    x_norm.moments(dve, t, lambda s: x1[:, r, s])
                    dve.wait_ge(s_xT, BASE + t)
                    x_norm.apply(dve, t, lambda s: x1[:, r, s], lambda s: xn[:, s])

                def split_x(t, r):
                    dve.wait_ge(s_xh, BASE + t + 1)
                    dve.tensor_tensor(xl[:, r], ps_x[:], xh[:, r].bitcast(F32), ALU.subtract).then_inc(s_xl, 1)

                def route(t):
                    dve.wait_ge(s_th, BASE + t + 1)
                    dve.tensor_scalar(sc[:], th[:], 0.5, 0.5, ALU.mult, ALU.add).then_inc(s_sc, 1)
                    dve.wait_ge(s_sc, BASE + t + 1)
                    for s in range(SUB):
                        last = dve.tensor_tensor(sel[:, s], sc[:, s], eb[:], ALU.add)
                    last.then_inc(s_sel, 1)
                    dve.wait_ge(s_sel, BASE + t + 1)
                    dve.memset(spare[:], 0.0)
                    for s in range(SUB):
                        last = dve.max(top[:, s], sel[:, s])
                    last.then_inc(s_top, 1)
                    dve.wait_ge(s_top, BASE + t + 1)
                    dve.memset(spare[:], 0.0)
                    for s in range(SUB):
                        last = dve.match_replace(rest[:, s], top[:, s], sel[:, s], -1e30)
                    last.then_inc(s_rest, 1)
                    dve.wait_ge(s_rest, BASE + t + 1)
                    dve.tensor_tensor(pick[:], rest[:], sel[:], ALU.not_equal).then_inc(s_pick, 1)
                    dve.wait_ge(s_pick, BASE + t + 1)
                    dve.tensor_tensor(part[:], pick[:], sc[:], ALU.mult).then_inc(s_part, 1)
                    dve.wait_ge(s_part, BASE + t + 1)
                    dve.tensor_reduce(tot[:], part[:], AX.X, ALU.add).then_inc(s_tot, 1)
                    dve.wait_ge(s_tot, BASE + t + 1)
                    dve.reciprocal(inv[:], tot[:]).then_inc(s_ti, 1)
                    dve.wait_ge(s_ti, BASE + t + 1)
                    for s in range(SUB):
                        last = dve.tensor_scalar(combine[:, bass.ds(t * SUB + s, 1), :], part[:, s:s + 1],
                                                 inv[:, s:s + 1], ROUTE_SCALE, ALU.mult, ALU.mult)
                    last.then_inc(s_c, 1)

                split_attn(0, 0)
                bias_and_norm(0, 0)

                def step(t, r, more):
                    if more:
                        split_attn(t + 1, 1 - r)
                    norm_x1(t, r)
                    if more:
                        bias_and_norm(t + 1, 1 - r)
                    dve.wait_ge(s_st[r], BASE + 48 * (t // 2))
                    split_x(t, r)
                    route(t)

                pipelined(dve, step)

            @block.scalar
            def _(act):
                act.wait_ge(s_w, BASE + 80)
                act.activation(wh[:], ws[:], ACT.Copy).then_inc(s_wh, 1)

                def attn_hi(t, r):
                    act.wait_ge(s_an, BASE + t + 1)
                    act.wait_ge(s_z, BASE + 2 * t)
                    act.activation(ah[:], an[:], ACT.Copy).then_inc(s_ah, 1)

                attn_hi(0, 0)

                def step(t, r, more):
                    if more:
                        attn_hi(t + 1, 1 - r)
                    act.wait_ge(s_xT, BASE + t + 1)
                    act.wait_ge(s_st[r], BASE + 48 * (t // 2))
                    act.activation(xh[:, r], ps_x[:], ACT.Copy).then_inc(s_xh, 1)
                    act.wait_ge(s_r, BASE + t + 1)
                    act.wait_ge(s_sc, BASE + t)
                    act.activation(th[:], ps_r[:], ACT.Tanh, scale=0.5).then_inc(s_th, 1)

                pipelined(act, step)

            @block.tensor
            def _(pe):
                pe.wait_ge(s_w, BASE + 80)
                pe.wait_ge(s_wl, BASE + 1)

                def project(t):
                    pe.wait_ge(s_al, BASE + t + 1)
                    pe.wait_ge(s_zb, BASE + 2 * t)
                    for s in range(SUB):
                        tok = slice(s * P, (s + 1) * P)
                        last = three_products(pe, ps_z[:, s], lambda c: ah[:, c, tok], lambda c: al[:, c, tok],
                                              lambda c: wh[:, c, 0:D], lambda c: wl[:, c, 0:D], KC)
                        if s % 2 == 1:
                            last.then_inc(s_z, 1)

                def transposes(t):
                    pe.wait_ge(x_norm.done, BASE + t + 1)
                    pe.wait_ge(s_xl, BASE + t)
                    for c in range(KC):
                        for s in range(SUB):
                            last = pe.transpose(ps_x[:, c, s * P:(s + 1) * P], xn[:, s, c * P:(c + 1) * P], ident[:])
                    last.then_inc(s_xT, 1)

                def router(t, r):
                    pe.wait_ge(s_xl, BASE + t + 1)
                    pe.wait_ge(s_th, BASE + t)
                    for s in range(SUB):
                        tok = slice(s * P, (s + 1) * P)
                        last = three_products(pe, ps_r[:, s], lambda c: xh[:, r, c, tok], lambda c: xl[:, r, c, tok],
                                              lambda c: wh[:, c, D:D + NE], lambda c: wl[:, c, D:D + NE], KC)
                    last.then_inc(s_r, 1)

                project(0)

                def step(t, r, more):
                    if more:
                        project(t + 1)
                    transposes(t)
                    router(t, r)

                pipelined(pe, step)



def experts(nc, outer, w_exp, w_sh, x1_dram, xT_dram, combine, out):
    with ExitStack() as inner:
        m = Mem(nc, outer, inner, "D")
        one = m.sb("one", [P, 1])
        ws = m.sb("w_stage", [P, 2, 3, KC, D])
        wh = m.sb("w_hi", [P, 2, 3, KC, D], F32R)
        wl = m.sb("w_lo", [P, 2, 3, KC, D], F32R)
        xh = m.sb("xT_hi", [P, GT, KC, TILE], F32R)
        xl = m.sb("xT_lo", [P, GT, KC, TILE], F32R)
        x1 = m.sb("x1", [P, GT, SUB, D])
        y = m.sb("y", [P, GT, SUB, D])
        yn = m.sb("y_normed", [P, SUB, D])
        ob = m.sb("out", [P, 2, SUB, D])
        th = m.sb("tanh", [P, KC, TILE])
        v = m.sb("gated", [P, KC, TILE])
        h = m.sb("hidden", [P, 2, KC, TILE])
        hh = m.sb("hidden_hi", [P, 2, KC, TILE], F32R)
        hl = m.sb("hidden_lo", [P, 2, KC, TILE], F32R)
        ps_g = m.ps("ps_gate", [P, KC, TILE])
        ps_u = m.ps("ps_up", [P, KC, TILE])
        ps_y = m.ps("ps_y", [P, 2, SUB, D])

        NW = NE + 1
        s_ws = [m.sem(f"w_loaded{i}", lifted=False) for i in range(2)]
        s_wh, s_wl, s_one = m.sem("w_hi"), m.sem("w_split"), m.sem("one")
        norm = Norm(m, "norm_y")
        s_x = [m.sem(f"xT_loaded{i}") for i in range(GT)]
        s_x1 = [m.sem(f"x1_loaded{i}") for i in range(GT)]
        s_gu, s_th, s_v, s_h, s_hh, s_hl = (m.sem(n) for n in (
            "hidden_products", "tanh", "gated", "hidden", "hidden_hi", "hidden_split"))
        s_yp, s_acc, s_ob = m.sem("y_products"), m.sem("accumulated"), m.sem("out_done")
        s_st = [m.sem(f"out_stored{i}") for i in range(2)]

        with nc.Block() as block:

            @block.sync
            def _(sp):
                def load_x1(g, tt):
                    sp.dma_start(x1[:, tt], x1_dram[bass.ds(g * GT + tt, 1)].rearrange("o p s d -> p (o s) d")
                                 ).then_inc(s_x1[tt], 16)

                for tt in range(GT):
                    load_x1(0, tt)

                def step(g, more):
                    for tt in range(GT):
                        sp.wait_ge(s_ob, BASE + g * GT + tt + 1)
                        sp.dma_start(out[bass.ds((g * GT + tt) * TILE, TILE), :].rearrange("(s p) d -> p s d", p=P),
                                     ob[:, tt % 2]).then_inc(s_st[tt % 2], 16)
                        if more:
                            load_x1(g + 1, tt)

                with sp.Fori(0, NGR - 1) as g:
                    step(g, True)
                step(NGR - 1, False)
                for i in range(2):
                    sp.wait_ge(s_st[i], BASE + 16 * NT // 2)

            @block.gpsimd
            def _(pool):
                def load(e, r):
                    src = w_sh if e is None else w_exp[bass.ds(e, 1)].rearrange("o p a c n -> p (o a) c n")
                    pool.dma_start(ws[:, r], src).then_inc(s_ws[r], 16)

                def split(w, r, first):
                    pool.wait_ge(s_ws[r], 16 * ((w - r) // 2 + 1))
                    if not first:
                        pool.wait_ge(s_yp, BASE + GT * (w - 1))
                    for a in range(3):
                        pool.tensor_tensor(wh[:, r, a].rearrange("p c n -> p (c n)"),
                                           ws[:, r, a].rearrange("p c n -> p (c n)"),
                                           one[:].broadcast_to((P, KC * D)), ALU.mult).then_inc(s_wh, 1)
                        pool.wait_ge(s_wh, BASE + 3 * w + a + 1)
                        pool.tensor_tensor(wl[:, r, a], ws[:, r, a], wh[:, r, a].bitcast(F32), ALU.subtract
                                           ).then_inc(s_wl, 1)
                    pool.wait_ge(s_wl, BASE + 3 * w + 3)

                def roots(g):
                    for tt in range(GT):
                        norm.root(pool, g * GT + tt)

                load(None, 0)
                load(0, 1)
                m.lift(pool)
                norm.constants(pool)
                pool.memset(one[:], 1.0).then_inc(s_one, 1)
                pool.wait_ge(s_one, BASE + 1)
                for g in range(NGR):
                    w = g * NW
                    split(w, w % 2, w < 2)
                    load(1, w % 2)
                    if g > 0:
                        roots(g - 1)
                    split(w + 1, (w + 1) % 2, w + 1 < 2)
                    load(2, (w + 1) % 2)
                    with pool.Fori(0, (NE - 4) // 2) as it:
                        for k in range(2):
                            r = (w + 2 + k) % 2
                            split(it * 2 + (w + 2 + k), r, False)
                            load(it * 2 + (3 + k), r)
                    for e in range(NE - 3, NE):
                        r = (w + 1 + e) % 2
                        split(w + 1 + e, r, False)
                        if e + 2 < NE:
                            load(e + 2, r)
                        elif g + 1 < NGR:
                            load(None if e + 2 == NE else 0, r)
                roots(NGR - 1)

            @block.vector
            def _(dve):

                def gate(n, tt):
                    r = tt % 2
                    for k in range(KC):
                        dve.wait_ge(s_th, BASE + KC * n + k + 1)
                        dve.scalar_tensor_tensor(v[:, k], th[:, k], 1.0, ps_g[:, k], ALU.add, ALU.mult).then_inc(s_v, 1)
                        dve.wait_ge(s_v, BASE + KC * n + k + 1)
                        dve.scalar_tensor_tensor(h[:, r, k], v[:, k], 0.5, ps_u[:, k], ALU.mult, ALU.mult
                                                 ).then_inc(s_h, 1)

                def low(n, tt):
                    r = tt % 2
                    for k in range(KC):
                        dve.wait_ge(s_hh, BASE + KC * n + k + 1)
                        dve.tensor_tensor(hl[:, r, k], h[:, r, k], hh[:, r, k].bitcast(F32), ALU.subtract
                                          ).then_inc(s_hl, 1)

                def accumulate(n, g, e, tt):
                    dve.wait_ge(s_yp, BASE + n + 1)
                    if e is None:
                        last = dve.tensor_copy(y[:, tt], ps_y[:, tt % 2])
                    else:
                        dve.wait_ge(s_acc, BASE + n - GT + 1)
                        for s in range(SUB):
                            c = combine[:, bass.ds((g * GT + tt) * SUB + s, 1), bass.ds(e, 1)].rearrange(
                                "p a b -> p (a b)")
                            last = dve.scalar_tensor_tensor(y[:, tt, s], ps_y[:, tt % 2, s], c, y[:, tt, s],
                                                            ALU.mult, ALU.add)
                    last.then_inc(s_acc, 1)

                def finish(g, tt):
                    t = g * GT + tt
                    dve.wait_ge(s_acc, BASE + (g * NW + NE) * GT + tt + 1)
                    norm.moments(dve, t, lambda s: y[:, tt, s])
                    norm.apply(dve, t, lambda s: y[:, tt, s], lambda s: yn[:, s])
                    dve.wait_ge(norm.done, BASE + t + 1)
                    dve.wait_ge(s_x1[tt], BASE + 16 * (g + 1))
                    dve.wait_ge(s_st[tt % 2], BASE + 16 * (g * 2 + tt // 2))
                    dve.tensor_tensor(ob[:, tt % 2], x1[:, tt], yn[:], ALU.add).then_inc(s_ob, 1)

                def ahead(n, tt, more=True):
                    if more:
                        gate(n + 1, (tt + 1) % GT)
                        low(n + 1, (tt + 1) % GT)

                def group(g, more):
                    for tt in range(GT):
                        n = g * (NW * GT) + tt
                        ahead(n, tt)
                        accumulate(n, g, None, tt)
                    with dve.Fori(0, NE - 1) as e:
                        for tt in range(GT):
                            n = g * (NW * GT) + (e + 1) * GT + tt
                            ahead(n, tt)
                            accumulate(n, g, e, tt)
                    for tt in range(GT):
                        n = g * (NW * GT) + NE * GT + tt
                        ahead(n, tt, more or tt < GT - 1)
                        accumulate(n, g, NE - 1, tt)
                        finish(g, tt)

                gate(0, 0)
                low(0, 0)
                with dve.Fori(0, NGR - 1) as g:
                    group(g, True)
                group(NGR - 1, False)

            @block.scalar
            def _(act):
                def load_x(g, tt):
                    for hl_, dst in enumerate((xh, xl)):
                        act.dma_start(dst[:, tt].bitcast(F32), xT_dram[bass.ds(g * GT + tt, 1), hl_].rearrange(
                            "o p c n -> p (o c) n")).then_inc(s_x[tt], 16)

                def tanh_and_hi(n, tt):
                    for k in range(KC):
                        act.wait_ge(s_gu, BASE + KC * n + k + 1)
                        act.wait_ge(s_v, BASE + KC * n)
                        act.activation(th[:, k], ps_g[:, k], ACT.Tanh, scale=0.5).then_inc(s_th, 1)
                    for k in range(KC):
                        act.wait_ge(s_h, BASE + KC * n + k + 1)
                        act.activation(hh[:, tt % 2, k], h[:, tt % 2, k], ACT.Copy).then_inc(s_hh, 1)

                for tt in range(GT):
                    load_x(0, tt)

                def group(g, more):
                    first = g * (NW * GT) + 1
                    with act.Fori(0, NE) as e:
                        for tt in range(GT):
                            tanh_and_hi(first + e * GT + tt, (tt + 1) % GT)
                    for tt in range(GT):
                        if more or tt < GT - 1:
                            tanh_and_hi(first + NE * GT + tt, (tt + 1) % GT)
                        if more:
                            load_x(g + 1, tt)

                tanh_and_hi(0, 0)
                with act.Fori(0, NGR - 1) as g:
                    group(g, True)
                group(NGR - 1, False)

            @block.tensor
            def _(pe):
                def hidden(n, w, r, tt):
                    if tt == 0:
                        pe.wait_ge(s_wl, BASE + 3 * w + 3)
                    pe.wait_ge(s_x[tt], BASE + 32 * (w // NW + 1))
                    pe.wait_ge(s_h, BASE + KC * n)
                    for k in range(KC):
                        cols = slice(k * P, (k + 1) * P)
                        for a, o in ((0, ps_g), (1, ps_u)):
                            last = three_products(pe, o[:, k], lambda c: wh[:, r, a, c, cols],
                                                  lambda c: wl[:, r, a, c, cols], lambda c: xh[:, tt, c],
                                                  lambda c: xl[:, tt, c], KC)
                        last.then_inc(s_gu, 1)

                def down(n, r, tt):
                    pe.wait_ge(s_hl, BASE + KC * n + KC)
                    if tt >= 2:
                        pe.wait_ge(s_acc, BASE + n - 1)
                    else:
                        pe.wait_ge(s_acc, BASE + n - tt)
                    b = tt % 2
                    for s in range(SUB):
                        tok = slice(s * P, (s + 1) * P)
                        last = three_products(pe, ps_y[:, b, s], lambda c: hh[:, b, c, tok], lambda c: hl[:, b, c, tok],
                                              lambda c: wh[:, r, 2, c], lambda c: wl[:, r, 2, c], KC)
                    last.then_inc(s_yp, 1)

                def expert(w, r, more):
                    for tt in range(GT):
                        n = w * GT + tt
                        if tt < GT - 1:
                            hidden(n + 1, w, r, tt + 1)
                        elif more:
                            hidden(n + 1, w + 1, 1 - r, 0)
                        down(n, r, tt)

                hidden(0, 0, 0, 0)
                with pe.Fori(0, NGR * NW // 2 - 1) as it:
                    for r in range(2):
                        expert(it * 2 + r, r, True)
                expert(NGR * NW - 2, 0, True)
                expert(NGR * NW - 1, 1, False)


def build(nc, x, w1, b1c, b1v, w2, b2, gate, ebias, w_exp, w_sh, ident, mask, maskT, out):
    qk = nc.dram_tensor("qk_scratch", (2, 2, B * D, S), F32, kind="Internal").ap()
    v = nc.dram_tensor("v_scratch", (NG, NBLK, P, HG * SLOT), F32, kind="Internal").ap()
    attn = nc.dram_tensor("attn_scratch", (B * D, S), F32, kind="Internal").ap()
    den = nc.dram_tensor("den_scratch", (B * H, S), F32, kind="Internal").ap()
    inv = nc.dram_tensor("inverse_scratch", (B * H, S), F32, kind="Internal").ap()
    x1 = nc.dram_tensor("x1_scratch", (NT, P, SUB, D), F32, kind="Internal").ap()
    xT = nc.dram_tensor("xT_scratch", (NT, 2, P, KC, TILE), F32, kind="Internal").ap()
    with ExitStack() as outer:
        combine = outer.enter_context(nc.sbuf_tensor("combine", [P, NT * SUB, NE], F32))
        project_qkv(nc, outer, x, w1, b1c, b1v, ident, qk, v)
        attention(nc, outer, ident, ident, mask, maskT, qk, v, attn, den)
        output_and_route(nc, outer, x, w2, b2, gate, ebias, ident, attn, den, inv, x1, xT, combine)
        experts(nc, outer, w_exp, w_sh, x1, xT, combine, out)


def kernel(L0_attn_x, L0_attn_W1, L0_attn_b1, L0_attn_W2, L0_attn_b2, L0_ffn_gate_w, L0_ffn_expert_bias,
           L0_ffn_w_gate, L0_ffn_w_up, L0_ffn_w_down, L0_ffn_shared_gate_w, L0_ffn_shared_up_w,
           L0_ffn_shared_down_w):
    import concourse.bacc as bacc
    from concourse.bass_utils import run_bass_kernel_spmd

    def rows(a):
        return np.broadcast_to(np.asarray(a)[None, :], (P, a.shape[-1]))

    def apart(a):
        return a.reshape(*a.shape[:-2], KC, P, a.shape[-1]).swapaxes(-3, -2)

    def weights(g, u, d):
        return np.stack([apart(np.swapaxes(w, -1, -2)) for w in map(np.asarray, (g, u, d))], axis=-4).swapaxes(-4, -3)

    w1 = np.asarray(L0_attn_W1).reshape(D, H, 3, DH).transpose(0, 2, 1, 3).reshape(D, 3 * D)
    b1 = np.asarray(L0_attn_b1).reshape(H, 3, DH).transpose(1, 0, 2).reshape(3 * D)
    i = np.arange(P)
    arrays = {
        "x": np.asarray(L0_attn_x).reshape(T, D), "w1": w1, "b1c": b1[:2 * D].reshape(4, P).T, "b1v": rows(b1[2 * D:]),
        "w2": np.asarray(L0_attn_W2), "b2": rows(L0_attn_b2), "gate": np.asarray(L0_ffn_gate_w).T,
        "ebias": rows(L0_ffn_expert_bias), "w_exp": weights(L0_ffn_w_gate, L0_ffn_w_up, L0_ffn_w_down),
        "w_sh": weights(L0_ffn_shared_gate_w, L0_ffn_shared_up_w, L0_ffn_shared_down_w),
        "ident": np.eye(P, dtype=np.float32),
        "mask": np.where(i[None, :] > i[:, None], MASK, 0.0).astype(np.float32),
        "maskT": np.where(i[None, :] < i[:, None], MASK, 0.0).astype(np.float32),
    }
    arrays = {f"in_{k}": np.ascontiguousarray(a) for k, a in arrays.items()}
    nc = bacc.Bacc("TRN2", target_bir_lowering=False, num_devices=1)
    aps = [nc.dram_tensor(k, a.shape, mybir.dt.from_np(a.dtype), kind="ExternalInput").ap() for k, a in arrays.items()]
    out = nc.dram_tensor("out", (T, D), F32, kind="ExternalOutput").ap()
    build(nc, *aps, out)
    got = run_bass_kernel_spmd(nc, [arrays], core_ids=[0]).results[0]["out"]
    return got.reshape(B, S, D)
```

```python
from contextlib import ExitStack

import numpy as np

import concourse.bass as bass
from concourse import mybir

ALU = mybir.AluOpType
ACT = mybir.ActivationFunctionType
AX = mybir.AxisListType
F32 = mybir.dt.float32
F32R = mybir.dt.float32r
BF16 = mybir.dt.bfloat16

P = 128
EPS = 1e-5
B, S, D, H, DH = 8, 1024, 256, 16, 16
T = B * S
TILE = 512
NT = T // TILE
SUB = TILE // P
KC = D // P
HG = 4
NGH = H // HG
NG = B * NGH
SLOT = 32
NBLK = S // P
NE, TOPK, F = 16, 8, 256
ROUTE_SCALE = 2.826
MASK = -4e10
GT = 4
BASE = 1
NGR = NT // GT


class Mem:

    def __init__(self, nc, outer, inner, stage):
        self.nc, self.outer, self.inner, self.stage = nc, outer, inner, stage
        self.sems = []

    def sb(self, name, shape, dt=F32):
        return self.inner.enter_context(self.nc.sbuf_tensor(f"{self.stage}_{name}", shape, dt))

    def ps(self, name, shape, dt=F32):
        return self.inner.enter_context(self.nc.psum_tensor(f"{self.stage}_{name}", shape, dt))

    def sem(self, name, lifted=True):
        s = self.outer.enter_context(self.nc.semaphore(f"{self.stage}_{name}"))
        if lifted:
            self.sems.append(s)
        return s

    def lift(self, eng):
        for s in self.sems:
            eng.sem_inc(s, BASE)


def three_products(pe, out, lhs_hi, lhs_lo, rhs_hi, rhs_lo, chunks):
    pairs = [(lhs_hi, rhs_hi), (lhs_hi, rhs_lo), (lhs_lo, rhs_hi)]
    last = None
    for c in range(chunks):
        for n, (a, b) in enumerate(pairs):
            last = pe.matmul(out, a(c), b(c), start=(c == 0 and n == 0), stop=(c == chunks - 1 and n == 2))
    return last


class Norm:

    def __init__(self, m, name):
        self.spare = m.sb(f"{name}_spare", [P, 1])
        self.const = m.sb(f"{name}_const", [P, 2])
        self.st = m.sb(f"{name}_stats", [P, SUB, 6])
        self.mv = m.sb(f"{name}_meanvar", [P, SUB, 2])
        self.ve = m.sb(f"{name}_var_eps", [P, SUB])
        self.rs = m.sb(f"{name}_rstd", [P, SUB])
        self.set, self.stats, self.aggr, self.added, self.power, self.done = (
            m.sem(f"{name}_{k}") for k in ("set", "stats", "aggr", "added", "power", "done"))

    def constants(self, pool):
        pool.memset(self.const[:, 0:1], EPS).then_inc(self.set, 1)
        pool.memset(self.const[:, 1:2], -0.5).then_inc(self.set, 1)
        pool.wait_ge(self.set, BASE + 2)

    def root(self, pool, t):
        pool.wait_ge(self.aggr, BASE + t + 1)
        pool.tensor_tensor(self.ve[:], self.mv[:, :, 1], self.const[:, 0:1].broadcast_to((P, SUB)), ALU.add
                           ).then_inc(self.added, 1)
        pool.wait_ge(self.added, BASE + t + 1)
        pool.wait_ge(self.done, BASE + t)
        pool.tensor_tensor(self.rs[:], self.ve[:], self.const[:, 1:2].broadcast_to((P, SUB)), ALU.pow
                           ).then_inc(self.power, 1)

    def moments(self, dve, t, src):
        for s in range(SUB):
            last = dve.bn_stats(self.st[:, s], src(s))
        last.then_inc(self.stats, 1)
        dve.wait_ge(self.stats, BASE + t + 1)
        dve.memset(self.spare[:], 0.0)
        for s in range(SUB):
            last = dve.bn_aggr(self.mv[:, s], self.st[:, s])
        last.then_inc(self.aggr, 1)

    def apply(self, dve, t, src, dst):
        dve.wait_ge(self.power, BASE + t + 1)
        for s in range(SUB):
            last = dve.tensor_scalar(dst(s), src(s), self.mv[:, s, 0:1], self.rs[:, s:s + 1],
                                     ALU.subtract, ALU.mult)
        last.then_inc(self.done, 1)


def half_count(t, r):
    return (t + 2 - r) // 2


def pipelined(eng, step):
    with eng.Fori(0, NT // 2 - 1) as it:
        for r in range(2):
            step(it * 2 + r, r, True)
    step(NT - 2, 0, True)
    step(NT - 1, 1, False)


def project_qkv(nc, outer, x, w1, b1c, b1v, ident_in, qk_dram, v_dram):
    with ExitStack() as inner:
        m = Mem(nc, outer, inner, "A")
        xt = m.sb("x", [P, 2, SUB, D])
        xn = m.sb("xn", [P, SUB, D])
        ident = m.sb("ident", [P, P])
        ws = m.sb("w_stage", [P, KC, 3 * D])
        wh = m.sb("w_hi", [P, KC, 3 * D], F32R)
        wl = m.sb("w_lo", [P, KC, 3 * D], F32R)
        bc = m.sb("bias_qk", [P, 4])
        bv = m.sb("bias_v", [P, D])
        xh = m.sb("xT_hi", [P, 2, KC, TILE], F32R)
        xl = m.sb("xT_lo", [P, 2, KC, TILE], F32R)
        qh = m.sb("qk_hi", [P, 2, 4, TILE], F32R)
        ql = m.sb("qk_lo", [P, 2, 4, TILE], F32R)
        vt = m.sb("v", [P, 2, SUB, H, SLOT])
        ps_x = m.ps("ps_xT", [P, KC, TILE])
        ps_q = m.ps("ps_qk", [P, 4, TILE])
        ps_v = m.ps("ps_v", [P, 2, 2, D])

        s_w, s_ones, s_wh, s_wsplit = m.sem("weights_loaded"), m.sem("ones"), m.sem("w_hi"), m.sem("w_split")
        s_x = [m.sem(f"x_loaded{i}") for i in range(2)]
        norm = Norm(m, "norm")
        s_xT, s_xh, s_xl = m.sem("transposed"), m.sem("xT_hi_done"), m.sem("xT_split")
        s_q, s_qh, s_ql = m.sem("qk_product"), m.sem("qk_hi_done"), m.sem("qk_split")
        s_v, s_vc = m.sem("v_product"), m.sem("v_copied")
        s_st = [m.sem(f"stored{i}") for i in range(2)]
        STORES = 4 * 2 + SUB

        with nc.Block() as block:

            @block.sync
            def _(sp):
                sp.dma_start(xt[:, 0], x[0:TILE, :].rearrange("(s p) d -> p s d", p=P)).then_inc(s_x[0], 16)
                sp.dma_start(ident[:], ident_in).then_inc(s_w, 16)
                sp.dma_start(ws[:], w1.rearrange("(c p) f -> p c f", p=P)).then_inc(s_w, 16)
                sp.dma_start(bc[:], b1c).then_inc(s_w, 16)
                sp.dma_start(bv[:], b1v).then_inc(s_w, 16)
                sp.dma_start(xt[:, 1], x[TILE:2 * TILE, :].rearrange("(s p) d -> p s d", p=P)).then_inc(s_x[1], 16)

                def step(t, r, more):
                    if more:
                        sp.wait_ge(norm.done, BASE + t + 1)
                        sp.dma_start(xt[:, r], x[bass.ds((t + 2) * TILE, TILE), :].rearrange(
                            "(s p) d -> p s d", p=P)).then_inc(s_x[r], 16)
                    b_, half = t // 2, r
                    for c in range(4):
                        sp.wait_ge(s_ql, BASE + 4 * t + c + 1)
                        for hl, src in enumerate((qh, ql)):
                            sp.dma_start(qk_dram[c // 2, hl, bass.ds(b_ * D + (c % 2) * P, P),
                                                 half * TILE:(half + 1) * TILE], src[:, r, c].bitcast(F32)).then_inc(s_st[r], 16)
                    sp.wait_ge(s_vc, BASE + 2 * t + 2)
                    for s in range(SUB):
                        sp.dma_start(v_dram[bass.ds(b_ * NGH, NGH), half * SUB + s].rearrange("g p f -> p g f"),
                                     vt[:, r, s].rearrange("p (g h) e -> p g (h e)", g=NGH)).then_inc(s_st[r], 16)

                with sp.Fori(0, NT // 2 - 1) as it:
                    for r in range(2):
                        step(it * 2 + r, r, True)
                step(NT - 2, 0, False)
                step(NT - 1, 1, False)
                for r in range(2):
                    sp.wait_ge(s_st[r], BASE + 16 * STORES * NT // 2)

            @block.gpsimd
            def _(pool):
                m.lift(pool)
                norm.constants(pool)
                norm.root(pool, 0)
                pipelined(pool, lambda t, r, more: norm.root(pool, t + 1) if more else None)

            @block.vector
            def _(dve):
                dve.wait_ge(s_w, BASE + 64)
                dve.wait_ge(s_wh, BASE + 1)
                dve.tensor_tensor(wl[:], ws[:], wh[:].bitcast(F32), ALU.subtract).then_inc(s_wsplit, 1)

                def front(t, r):
                    dve.wait_ge(s_x[r], BASE + (t // 2 + 1) * 16)
                    norm.moments(dve, t, lambda s: xt[:, r, s])
                    dve.wait_ge(s_xT, BASE + t)
                    norm.apply(dve, t, lambda s: xt[:, r, s], lambda s: xn[:, s])

                def split(t, r):
                    dve.wait_ge(s_xh, BASE + t + 1)
                    dve.tensor_tensor(xl[:, r], ps_x[:], xh[:, r].bitcast(F32), ALU.subtract).then_inc(s_xl, 1)

                def step(t, r, more):
                    if more:
                        front(t + 1, 1 - r)
                    for c in range(4):
                        dve.wait_ge(s_qh, BASE + 4 * t + c + 1)
                        dve.scalar_tensor_tensor(ql[:, r, c], ps_q[:, c], bc[:, c:c + 1], qh[:, r, c].bitcast(F32),
                                                 ALU.add, ALU.subtract).then_inc(s_ql, 1)
                    if more:
                        split(t + 1, 1 - r)
                    dve.wait_ge(s_st[r], BASE + (t // 2) * 16 * STORES)
                    for k in range(2):
                        dve.wait_ge(s_v, BASE + 2 * t + k + 1)
                        for j in range(2):
                            s = 2 * k + j
                            last = dve.tensor_tensor(vt[:, r, s, :, 0:DH],
                                                     ps_v[:, k, j].rearrange("p (h e) -> p h e", h=H),
                                                     bv[:].rearrange("p (h e) -> p h e", h=H), ALU.add)
                        last.then_inc(s_vc, 1)

                dve.memset(vt[:, :, :, :, DH:SLOT], 1.0).then_inc(s_ones, 1)
                front(0, 0)
                split(0, 0)
                pipelined(dve, step)

            @block.scalar
            def _(act):
                act.wait_ge(s_w, BASE + 64)
                act.activation(wh[:], ws[:], ACT.Copy).then_inc(s_wh, 1)

                def split(t, r):
                    act.wait_ge(s_xT, BASE + t + 1)
                    act.activation(xh[:, r], ps_x[:], ACT.Copy).then_inc(s_xh, 1)

                def step(t, r, more):
                    act.wait_ge(s_st[r], BASE + (t // 2) * 16 * STORES)
                    for c in range(4):
                        act.wait_ge(s_q, BASE + 4 * t + c + 1)
                        act.activation(qh[:, r, c], ps_q[:, c], ACT.Identity, bias=bc[:, c:c + 1]).then_inc(s_qh, 1)
                    if more:
                        split(t + 1, 1 - r)

                split(0, 0)
                pipelined(act, step)

            @block.tensor
            def _(pe):
                pe.wait_ge(s_w, BASE + 64)

                def transposes(t):
                    pe.wait_ge(norm.done, BASE + t + 1)
                    pe.wait_ge(s_xl, BASE + t)
                    for c in range(KC):
                        for s in range(SUB):
                            last = pe.transpose(ps_x[:, c, s * P:(s + 1) * P], xn[:, s, c * P:(c + 1) * P], ident[:])
                    last.then_inc(s_xT, 1)

                def step(t, r, more):
                    pe.wait_ge(s_xl, BASE + t + 1)
                    for c in range(4):
                        pe.wait_ge(s_ql, BASE + 4 * t)
                        three_products(pe, ps_q[:, c], lambda k: wh[:, k, c * P:(c + 1) * P],
                                       lambda k: wl[:, k, c * P:(c + 1) * P], lambda k: xh[:, r, k],
                                       lambda k: xl[:, r, k], KC).then_inc(s_q, 1)
                    if more:
                        transposes(t + 1)
                    for k2 in range(2):
                        pe.wait_ge(s_vc, BASE + 2 * t)
                        for j in range(2):
                            s = 2 * k2 + j
                            last = three_products(pe, ps_v[:, k2, j], lambda k: xh[:, r, k, s * P:(s + 1) * P],
                                                  lambda k: xl[:, r, k, s * P:(s + 1) * P],
                                                  lambda k: wh[:, k, 2 * D:3 * D], lambda k: wl[:, k, 2 * D:3 * D], KC)
                        last.then_inc(s_v, 1)

                transposes(0)
                pe.wait_ge(s_wsplit, BASE + 1)
                pipelined(pe, step)


WIDE = [(i, (h,)) for i in range(4, NBLK) for h in range(HG)]
NARROW = {i: [(i, (h, h + 1)) for h in (0, 2)] for i in range(4)}
UNITS = WIDE[:2] + NARROW[3] + NARROW[1] + WIDE[2:6] + NARROW[2] + NARROW[0] + WIDE[6:]
FIRST = len(UNITS)
KEYS = [(qh, j) for qh in range(2) for j in range(4 * (qh + 1))]
QUADS = len(KEYS)
SLOTS = 3
STACK = 3 * DH
PAD = 96
SHIFT = PAD + 2
HALF = KEYS.index((1, 0))
EARLY = 8
MAX_AT = 2 + FIRST - EARLY + 1


def width(qh, j):
    return TILE - max(0, j * P - qh * TILE)


def schedule():
    units = []
    for k in range(2 * QUADS):
        units.append(("second", 2 + k))
        if k < FIRST - EARLY:
            units.append(("next", EARLY + k))
        else:
            units.append(("after", k - (FIRST - EARLY)))
    return units


def attention(nc, outer, ident_in, identb_in, mask_in, maskT_in, qk_dram, v_dram, a_dram, den_dram):
    with ExitStack() as inner:
        m = Mem(nc, outer, inner, "B")
        qs = m.sb("q_stack", [P, 3, HG, S], F32R)
        ks = m.sb("k_stack", [P, 3, HG, S], F32R)
        vs = m.sb("v", [P, 3, NBLK, HG * SLOT])
        pt = m.sb("probs", [P, SLOTS, HG, TILE])
        mx = m.sb("max", [P, 3, HG, NBLK])
        mh = m.sb("neg_max_hi", [HG * NBLK, P], F32R)
        ml = m.sb("neg_max_lo", [HG * NBLK, P], F32R)
        ident = m.sb("ident", [P, P])
        identr = m.sb("ident_r", [P, P], F32R)
        mask = m.sb("mask", [P, P], F32R)
        maskT = m.sb("maskT", [P, P], F32R)
        on = m.sb("out_raw", [P, 2, TILE])
        stage = m.sb("mask_stage", [P, 3, P])
        ps = m.ps("slots", [P, SLOTS, 2 * TILE])
        po = m.ps("ps_out", [P, TILE])
        pm = m.ps("ps_maxT", [P, TILE])

        s_c, s_set, s_kset = m.sem("constants_loaded"), m.sem("constants_set"), m.sem("k_constants_set")
        s_ld = [m.sem(f"group_loaded{i}") for i in range(3)]
        s_sc1, s_max = m.sem("first_scores"), m.sem("first_max")
        s_mT, s_mh, s_ml, s_row = m.sem("maxT"), m.sem("neg_max_hi"), m.sem("neg_max"), m.sem("max_rows")
        s_sc2, s_exp = m.sem("second_scores"), m.sem("exped")
        s_pfree = m.sem("probs_free")
        s_on = m.sem("out_raw")
        s_st = [m.sem(f"out_stored{i}") for i in range(2)]
        LOADS, STORES = 7, 16 * 2 * HG
        sched = schedule()

        def in_loop(eng, step):
            with eng.Fori(0, NG // 3) as it:
                for r in range(3):
                    step(it * 3 + r, r, True, True)
            step(NG - 2, 0, True, False)
            step(NG - 1, 1, False, False)

        with nc.Block() as block:

            @block.sync
            def _(sp):
                def load(g, r):
                    for row, hl in ((0, 0), (1, 1), (2, 0)):
                        sp.dma_start(qs[row * DH:(row + 1) * DH, r].bitcast(F32), qk_dram[
                            0, hl, bass.ds(g * HG * DH, HG * DH), :].rearrange("(h d) n -> d h n", d=DH)
                        ).then_inc(s_ld[r], 16)
                    for row, hl in ((0, 0), (1, 0), (2, 1)):
                        sp.dma_start(ks[row * DH:(row + 1) * DH, r].bitcast(F32), qk_dram[
                            1, hl, bass.ds(g * HG * DH, HG * DH), :].rearrange("(h d) n -> d h n", d=DH)
                        ).then_inc(s_ld[r], 16)
                    sp.dma_start(vs[:, r], v_dram[bass.ds(g, 1)].rearrange("o j p f -> p (o j) f")
                                 ).then_inc(s_ld[r], 16)

                def max_rows(g, r):
                    sp.wait_ge(s_ml, BASE + g + 1)
                    for row, src in ((PAD, mh), (PAD + 1, ml)):
                        sp.dma_start(qs[row:row + 1, r].bitcast(F32).rearrange("o h (i q) -> o (h i) q", q=P),
                                     src[:].bitcast(F32)).then_inc(s_row, 16)

                def store(g, qh):
                    sp.wait_ge(s_on, BASE + 2 * g + qh + 1)
                    for h in range(HG):
                        sp.dma_start(a_dram[bass.ds(g * HG * DH + h * DH, DH), qh * TILE:(qh + 1) * TILE],
                                     on[h * SLOT:h * SLOT + DH, qh]).then_inc(s_st[qh], 16)
                        sp.dma_start(den_dram[bass.ds(g * HG + h, 1), qh * TILE:(qh + 1) * TILE],
                                     on[h * SLOT + DH:h * SLOT + DH + 1, qh]).then_inc(s_st[qh], 16)

                sp.dma_start(ident[:], ident_in).then_inc(s_c, 16)
                sp.dma_start(stage[:, 0], identb_in).then_inc(s_c, 16)
                sp.dma_start(stage[:, 1], mask_in).then_inc(s_c, 16)
                sp.dma_start(stage[:, 2], maskT_in).then_inc(s_c, 16)
                sp.wait_ge(s_set, BASE + 1)
                for r in range(3):
                    sp.wait_ge(s_kset, BASE + 2 + 3 * r)
                    load(r, r)
                max_rows(0, 0)

                def step(g, r, more, loads):
                    if more:
                        max_rows(g + 1, (r + 1) % 3)
                    store(g, 0)
                    if loads:
                        sp.wait_ge(s_pfree, BASE + SLOTS + (g + 1) * QUADS)
                        load(g + 3, r)
                    store(g, 1)

                with sp.Fori(0, NG // 3 - 1) as it:
                    for r in range(3):
                        step(it * 3 + r, r, True, True)
                for g in range(NG // 3 * 3 - 3, NG):
                    step(g, g % 3, g + 1 < NG, g + 3 < NG)
                for qh in range(2):
                    sp.wait_ge(s_st[qh], BASE + NG * STORES)

            @block.gpsimd
            def _(pool):
                m.lift(pool)
                for r in range(3):
                    if r > 0:
                        pool.wait_ge(s_kset, BASE + 3 * r - 1)
                        pool.memset(qs[:, r].bitcast(F32), 0.0).then_inc(s_kset, 1)
                        pool.wait_ge(s_kset, BASE + 3 * r)
                    pool.memset(ks[0:PAD, r].bitcast(F32), 0.0).then_inc(s_kset, 1)
                    pool.wait_ge(s_kset, BASE + 3 * r + 1)
                    pool.memset(ks[PAD:P, r].bitcast(F32), 1.0).then_inc(s_kset, 1)

            @block.vector
            def _(dve):
                dve.memset(qs[:, 0].bitcast(F32), 0.0).then_inc(s_set, 1)
                dve.wait_ge(s_c, BASE + 64)
                dve.tensor_copy(identr[:], stage[:, 0]).then_inc(s_set, 1)
                dve.tensor_copy(mask[:], stage[:, 1]).then_inc(s_set, 1)
                dve.tensor_copy(maskT[:], stage[:, 2]).then_inc(s_set, 1)

                def maxima(g, r, u, slot):
                    i, heads = UNITS[u]
                    w = (i + 1) * P
                    dve.wait_ge(s_sc1, BASE + g * FIRST + u + 1)
                    if len(heads) == 2:
                        src = ps[:, slot].rearrange("p (h n) -> p h n", h=2)[:, :, 0:w]
                    else:
                        src = ps[:, slot, 0:w]
                    dve.tensor_reduce(mx[:, r, heads[0]:heads[-1] + 1, i], src, AX.X, ALU.max).then_inc(s_max, 1)

                def rows(g):
                    dve.wait_ge(s_mT, BASE + g + 1)
                    dve.wait_ge(s_row, BASE + 32 * g)
                    n = HG * NBLK
                    dve.tensor_scalar(mh[:], pm[0:n, 0:P], -1.0, None, ALU.mult).then_inc(s_mh, 1)
                    dve.wait_ge(s_mh, BASE + g + 1)
                    dve.scalar_tensor_tensor(ml[:], pm[0:n, 0:P], -1.0, mh[:].bitcast(F32), ALU.mult,
                                             ALU.subtract).then_inc(s_ml, 1)

                for u in range(FIRST):
                    maxima(0, 0, u, u % SLOTS)
                for u in range(EARLY):
                    maxima(1, 1, u, u % SLOTS)
                    if u == 1:
                        rows(0)

                def step(g, r, next_, after):
                    for n, (kind, u) in enumerate(sched):
                        if kind == "next" and next_:
                            maxima(g + 1, (r + 1) % 3, u, n % SLOTS)
                        if kind == "after" and after:
                            maxima(g + 2, (r + 2) % 3, u, n % SLOTS)
                        if (kind, u) == ("after", 0) and next_:
                            rows(g + 1)

                in_loop(dve, step)

            @block.scalar
            def _(act):
                def exps(g, v, slot):
                    qh, j = KEYS[v // 2 % QUADS]
                    buf = v // 2 % SLOTS
                    w = width(qh, j)
                    act.wait_ge(s_sc2, BASE + g * 2 * QUADS + v + 1)
                    if v % 2 == 0:
                        act.wait_ge(s_pfree, BASE + g * QUADS + v // 2 + 1)
                    h = v % 2 * 2
                    act.activation(pt[:, buf, h:h + 2, 0:w], ps[:, slot].rearrange("p (h n) -> p h n", h=2)[:, :, 0:w],
                                   ACT.Exp, scale=float(DH) ** -0.5).then_inc(s_exp, 1)

                def raw(g, qh):
                    act.wait_ge(s_pfree, BASE + SLOTS + g * QUADS + (QUADS if qh else HALF))
                    act.wait_ge(s_st[qh], BASE + g * STORES)
                    act.activation(on[:, qh], po[:], ACT.Copy).then_inc(s_on, 1)

                for v in range(2):
                    exps(0, v, (2 * (v - 2)) % SLOTS)

                def step(g, r, more, after):
                    for n, (kind, v) in enumerate(sched):
                        if kind == "second" and (more or v < 2 * QUADS):
                            exps(g, v, n % SLOTS)
                        if (kind, v) == ("second", 2 * HALF + 2):
                            raw(g, 0)
                    raw(g, 1)

                in_loop(act, step)

            @block.tensor
            def _(pe):
                pe.sem_inc(s_pfree, SLOTS)
                pe.wait_ge(s_set, BASE + 4)

                def first(g, r, u, slot):
                    i, heads = UNITS[u]
                    w = (i + 1) * P
                    for b, h in enumerate(heads):
                        o = ps[:, slot, b * TILE:(b + 1) * TILE]
                        q = qs[0:PAD, r, h, i * P:(i + 1) * P]
                        if w > TILE:
                            pe.matmul(o, q, ks[0:PAD, r, h, 0:TILE], start=True, stop=True)
                            o = ps[:, slot, TILE:2 * TILE]
                            pe.matmul(o[:, 0:w - TILE], q, ks[0:PAD, r, h, TILE:w], start=True, stop=False)
                        else:
                            pe.matmul(o[:, 0:w], q, ks[0:PAD, r, h, 0:w], start=True, stop=False)
                        at = (w - P) % TILE
                        last = pe.matmul(o[:, at:at + P], identr[:], mask[:], start=False, stop=True)
                    last.then_inc(s_sc1, 1)

                def second(g, r, v, slot):
                    qh, j = KEYS[v // 2 % QUADS]
                    w = width(qh, j)
                    q0 = (qh + 1) * TILE - w
                    for b in range(2):
                        h = v % 2 * 2 + b
                        o = ps[:, slot, b * TILE:b * TILE + w]
                        diagonal = q0 == j * P
                        last = pe.matmul(o, ks[0:SHIFT, r, h, j * P:(j + 1) * P], qs[0:SHIFT, r, h, q0:q0 + w],
                                         start=True, stop=not diagonal)
                        if diagonal:
                            last = pe.matmul(o[:, 0:P], identr[:], maskT[:], start=False, stop=True)
                    last.then_inc(s_sc2, 1)

                def values(g, r, k):
                    qh, j = KEYS[k]
                    w = width(qh, j)
                    pe.wait_ge(s_exp, BASE + g * 2 * QUADS + 2 * k + 2)
                    if j == 0:
                        pe.wait_ge(s_on, BASE + 2 * g + qh)
                    for h in range(HG):
                        last = pe.matmul(po[h * SLOT:(h + 1) * SLOT, TILE - w:TILE], vs[:, r, j, h * SLOT:(h + 1) * SLOT],
                                         pt[:, k % SLOTS, h, 0:w], start=(j == 0), stop=(j == 4 * (qh + 1) - 1))
                    last.then_inc(s_pfree, 1)

                def max_transpose(g, r):
                    pe.wait_ge(s_max, BASE + (g + 1) * FIRST)
                    pe.wait_ge(s_ml, BASE + g)
                    pe.transpose(pm[0:HG * NBLK, 0:P], mx[:, r].rearrange("p h i -> p (h i)"), ident[:]).then_inc(s_mT, 1)

                def group_loaded(g, r):
                    pe.wait_ge(s_ld[r], BASE + ((g - r) // 3 + 1) * 16 * LOADS)

                group_loaded(0, 0)
                for u in range(FIRST):
                    if u >= SLOTS:
                        pe.wait_ge(s_max, BASE + u - SLOTS + 1)
                    first(0, 0, u, u % SLOTS)
                group_loaded(1, 1)
                for u in range(EARLY):
                    pe.wait_ge(s_max, BASE + FIRST + u - SLOTS + 1)
                    first(1, 1, u, u % SLOTS)
                    if u == 1:
                        max_transpose(0, 0)
                pe.wait_ge(s_max, BASE + FIRST + EARLY)
                pe.wait_ge(s_row, BASE + 32)
                for v in range(2):
                    second(0, 0, v, (2 * (v - 2)) % SLOTS)

                def slot_free(g, n, next_, after):
                    for p in (n - SLOTS, n - 2 * SLOTS):
                        back = 1 if p < 0 else 0
                        kind, u = sched[p]
                        if kind == "second":
                            pe.wait_ge(s_exp, BASE + (g - back) * 2 * QUADS + u + 1)
                            return
                        if kind == "next" and (next_ or back):
                            pe.wait_ge(s_max, BASE + (g + 1 - back) * FIRST + u + 1)
                            return
                        if kind == "after" and (next_ if back else after):
                            pe.wait_ge(s_max, BASE + (g + 2 - back) * FIRST + u + 1)
                            return

                def step(g, r, next_, after):
                    for n, (kind, u) in enumerate(sched):
                        if kind == "next":
                            if next_:
                                slot_free(g, n, next_, after)
                                first(g + 1, (r + 1) % 3, u, n % SLOTS)
                            continue
                        if kind == "after":
                            if after:
                                if u == 0:
                                    group_loaded(g + 2, (r + 2) % 3)
                                slot_free(g, n, next_, after)
                                first(g + 2, (r + 2) % 3, u, n % SLOTS)
                            continue
                        if u < 2 * QUADS:
                            slot_free(g, n, next_, after)
                            second(g, r, u, n % SLOTS)
                        elif next_:
                            slot_free(g, n, next_, after)
                            if u == 2 * QUADS:
                                pe.wait_ge(s_row, BASE + 32 * (g + 2))
                            second(g + 1, (r + 1) % 3, u - 2 * QUADS, n % SLOTS)
                        if u % 2 == 1:
                            values(g, r, u // 2 - 1)
                        if next_ and u == MAX_AT:
                            max_transpose(g + 1, (r + 1) % 3)

                in_loop(pe, step)


class FoldedNorm:

    def __init__(self, m, name):
        self.spare = m.sb(f"{name}_spare", [P, 1])
        self.const = m.sb(f"{name}_const", [P, 3])
        self.st = m.sb(f"{name}_stats", [P, SUB, 6])
        self.mv = m.sb(f"{name}_meanvar", [P, SUB, 2])
        self.ve = m.sb(f"{name}_var_eps", [P, SUB])
        self.nm = m.sb(f"{name}_neg_mean", [P, SUB])
        self.rs = m.sb(f"{name}_rstd", [P, SUB])
        self.sh = m.sb(f"{name}_shift", [P, SUB])
        self.set, self.stats, self.aggr, self.added, self.power, self.shift, self.done = (
            m.sem(f"{name}_{k}") for k in ("set", "stats", "aggr", "added", "power", "shift", "done"))

    def constants(self, pool):
        for n, value in enumerate((EPS, -0.5, -1.0)):
            pool.memset(self.const[:, n:n + 1], value).then_inc(self.set, 1)
        pool.wait_ge(self.set, BASE + 3)

    def root(self, pool, t):
        pool.wait_ge(self.aggr, BASE + t + 1)
        pool.tensor_tensor(self.ve[:], self.mv[:, :, 1], self.const[:, 0:1].broadcast_to((P, SUB)), ALU.add
                           ).then_inc(self.added, 1)
        pool.tensor_tensor(self.nm[:], self.mv[:, :, 0], self.const[:, 2:3].broadcast_to((P, SUB)), ALU.mult
                           ).then_inc(self.added, 1)
        pool.wait_ge(self.added, BASE + 2 * t + 2)
        pool.wait_ge(self.done, BASE + t)
        pool.tensor_tensor(self.rs[:], self.ve[:], self.const[:, 1:2].broadcast_to((P, SUB)), ALU.pow
                           ).then_inc(self.power, 1)
        pool.wait_ge(self.power, BASE + t + 1)
        pool.tensor_tensor(self.sh[:], self.nm[:], self.rs[:], ALU.mult).then_inc(self.shift, 1)

    def moments(self, dve, t, src):
        for s in range(SUB):
            last = dve.bn_stats(self.st[:, s], src(s))
        last.then_inc(self.stats, 1)
        dve.wait_ge(self.stats, BASE + t + 1)
        dve.wait_ge(self.added, BASE + 2 * t)
        dve.memset(self.spare[:], 0.0)
        for s in range(SUB):
            last = dve.bn_aggr(self.mv[:, s], self.st[:, s])
        last.then_inc(self.aggr, 1)

    def apply(self, act, t, src, dst):
        act.wait_ge(self.shift, BASE + t + 1)
        for s in range(SUB):
            last = act.activation(dst(s), src(s), ACT.Identity, bias=self.sh[:, s:s + 1], scale=self.rs[:, s:s + 1])
        last.then_inc(self.done, 1)


def output_and_route(nc, outer, x, w2, b2, gate, ebias, ident_in, spread_in, a_dram, den_dram,
                     x1_dram, xT_dram, combine):
    AHEAD, LAG = 4, 2
    PAIR = 2 * SUB
    with ExitStack() as inner:
        m = Mem(nc, outer, inner, "C")
        at = m.sb("attnT", [P, 2, KC, TILE])
        den = m.sb("denominators", [P, S])
        dp = m.sb("inverse_parts", [P, 3, S], BF16)
        rem = m.sb("inverse_rest", [P, S])
        spread = m.sb("spread", [P, NT, P], BF16)
        ss = m.sb("spread_stage", [P, NT, P])
        an = m.sb("attnT_normed", [P, KC, TILE])
        ah = m.sb("attnT_hi", [P, 2, KC, TILE], F32R)
        al = m.sb("attnT_lo", [P, 2, KC, TILE], F32R)
        xt = m.sb("x", [P, 2, SUB, D])
        zn = m.sb("z_normed", [P, SUB, D])
        x1 = m.sb("x1", [P, 2, SUB, D])
        xn = m.sb("x1_normed", [P, SUB, D])
        xh = m.sb("xT_hi", [P, 2, KC, TILE], F32R)
        xl = m.sb("xT_lo", [P, 2, KC, TILE], F32R)
        ws = m.sb("w_stage", [P, KC, D + NE])
        wh = m.sb("w_hi", [P, KC, D + NE], F32R)
        wl = m.sb("w_lo", [P, KC, D + NE], F32R)
        ones = m.sb("ones", [P, P], F32R)
        bs = m.sb("bias_stage", [P, D])
        bb = m.sb("bias_out", [P, D], F32R)
        eb = m.sb("bias_expert", [P, PAIR, NE])
        ident = m.sb("ident", [P, P])
        spare = m.sb("spare", [P, 1])
        th = m.sb("tanh", [P, PAIR, NE])
        sc = m.sb("scores", [P, PAIR, NE])
        sel = m.sb("scores_biased", [P, PAIR, NE])
        top = m.sb("top8", [P, PAIR, TOPK])
        rest = m.sb("rest", [P, PAIR, NE])
        pick = m.sb("picked", [P, PAIR, NE])
        part = m.sb("picked_scores", [P, PAIR, NE])
        tot = m.sb("picked_sum", [P, PAIR])
        inv = m.sb("picked_inverse", [P, PAIR])
        ps_i = m.ps("ps_inverses", [P, KC, TILE])
        ps_z = m.ps("ps_z", [P, SUB, D])
        ps_x = m.ps("ps_xT", [P, KC, TILE])
        ps_r = m.ps("ps_router", [P, SUB, NE])

        s_w, s_bz, s_b, s_wh, s_wl = (m.sem(n) for n in ("weights_loaded", "bias_zeros", "bias_loaded", "w_hi", "w_split"))
        s_den, s_sp, s_spread, s_inv = (m.sem(n) for n in ("den_loaded", "spread_loaded", "spread_bf", "inverses"))
        z_norm, x_norm = FoldedNorm(m, "norm_z"), FoldedNorm(m, "norm_x1")
        s_la = [m.sem(f"attn_loaded{i}") for i in range(2)]
        s_lx = [m.sem(f"x_loaded{i}") for i in range(2)]
        s_i, s_an, s_ah, s_al, s_z, s_x1 = (m.sem(n) for n in (
            "inverses_spread", "attnT_normed", "attnT_hi", "attnT_split", "z", "x1_done"))
        s_xT, s_xh, s_xl, s_r = (m.sem(n) for n in ("transposed", "xT_hi", "xT_split", "router_product"))
        s_th, s_sc, s_sel, s_top, s_rest, s_pick, s_part, s_tot, s_ti, s_c = (m.sem(n) for n in (
            "tanh", "scores", "biased", "top8", "rest", "picked", "picked_scores", "picked_sum", "sum_inverse", "combine"))
        s_sx, s_sT = ([m.sem(f"{n}_stored{i}") for i in range(2)] for n in ("x1", "xT"))

        def there(t):
            return not isinstance(t, int) or 0 <= t < NT

        def steps(eng, step):
            for t in range(-AHEAD, LAG):
                step(t, t % 2)
            pairs = (NT - AHEAD - LAG) // 2
            with eng.Fori(0, pairs) as it:
                for r in range(2):
                    step(it * 2 + LAG + r, (LAG + r) % 2)
            for t in range(LAG + 2 * pairs, NT + LAG):
                step(t, t % 2)

        with nc.Block() as block:

            @block.sync
            def _(sp):
                def load_attn(t, r):
                    half = t % 2 if isinstance(t, int) else r
                    base = t // 2 * D if isinstance(t, int) else (t - half) * (D // 2)
                    sp.dma_start(at[:, r], a_dram[bass.ds(base, D), half * TILE:(half + 1) * TILE].rearrange(
                        "(c p) n -> p c n", p=P)).then_inc(s_la[r], 16)

                def load_x(t, r):
                    sp.dma_start(xt[:, r], x[bass.ds(t * TILE, TILE), :].rearrange("(s p) d -> p s d", p=P)
                                 ).then_inc(s_lx[r], 16)

                sp.dma_start(den[:], den_dram).then_inc(s_den, 16)
                load_attn(0, 0)
                sp.dma_start(ss[:].rearrange("p t m -> p (t m)"), spread_in).then_inc(s_sp, 16)
                sp.dma_start(ws[:, :, 0:D], w2.rearrange("(c p) f -> p c f", p=P)).then_inc(s_w, 16)
                sp.dma_start(ws[:, :, D:D + NE], gate.rearrange("(c p) f -> p c f", p=P)).then_inc(s_w, 16)
                sp.dma_start(eb[:].rearrange("p s e -> p (s e)"), ebias).then_inc(s_w, 16)
                sp.dma_start(ident[:], ident_in).then_inc(s_w, 16)
                sp.wait_ge(s_bz, BASE + 1)
                for row in (0, 32):
                    sp.dma_start(bs[row:row + 1], b2[0:1, :]).then_inc(s_b, 16)
                load_attn(1, 1)
                load_x(0, 0)
                load_x(1, 1)

                def step(t, r):
                    if there(t + 4) and not (isinstance(t, int) and t + 4 < 2):
                        sp.wait_ge(s_an, BASE + t + 3)
                        load_attn(t + 4, r)
                    if there(t - 1):
                        sp.wait_ge(s_xl, BASE + t)
                        for hl, src in enumerate((xh, xl)):
                            sp.dma_start(xT_dram[bass.ds(t - 1, 1), hl].rearrange("o p c n -> p (o c) n"),
                                         src[:, 1 - r].bitcast(F32)).then_inc(s_sT[1 - r], 16)
                    if there(t):
                        sp.wait_ge(s_x1, BASE + t + 1)
                        if there(t + 2):
                            load_x(t + 2, r)
                        sp.dma_start(x1_dram[bass.ds(t, 1)].rearrange("o p s d -> p (o s) d"), x1[:, r]).then_inc(s_sx[r], 16)

                steps(sp, step)
                for r in range(2):
                    sp.wait_ge(s_sx[r], BASE + 16 * NT // 2)
                    sp.wait_ge(s_sT[r], BASE + 32 * NT // 2)

            @block.gpsimd
            def _(pool):
                m.lift(pool)
                pool.memset(bs[:], 0.0).then_inc(s_bz, 1)
                z_norm.constants(pool)
                x_norm.constants(pool)

                def step(t, r):
                    if there(t + 1):
                        z_norm.root(pool, t + 1)
                    if there(t):
                        x_norm.root(pool, t)
                    if there(t + 1):
                        pool.wait_ge(s_lx[1 - r], BASE + 16 * half_count(t + 1, 1 - r))
                        pool.wait_ge(z_norm.done, BASE + t + 2)
                        if there(t - 1):
                            pool.wait_ge(s_sx[1 - r], BASE + 16 * half_count(t - 1, 1 - r))
                        pool.tensor_tensor(x1[:, 1 - r], xt[:, 1 - r], zn[:], ALU.add).then_inc(s_x1, 1)

                steps(pool, step)

            @block.vector
            def _(dve):
                dve.wait_ge(s_den, BASE + 16)
                dve.reciprocal(den[:], den[:]).then_inc(s_inv, 1)
                for n, part_of in enumerate((den, rem, rem)):
                    dve.wait_ge(s_inv, BASE + 2 * n + 1)
                    dve.tensor_copy(dp[:, n], part_of[:]).then_inc(s_inv, 1)
                    if n < 2:
                        dve.wait_ge(s_inv, BASE + 2 * n + 2)
                        dve.tensor_tensor(rem[:], part_of[:], dp[:, n], ALU.subtract).then_inc(s_inv, 1)
                dve.wait_ge(s_w, BASE + 64)
                dve.tensor_scalar(ones[:], ident[:], 0.0, 1.0, ALU.mult, ALU.add).then_inc(s_wl, 1)
                dve.wait_ge(s_wh, BASE + 1)
                dve.tensor_tensor(wl[:], ws[:], wh[:].bitcast(F32), ALU.subtract).then_inc(s_wl, 1)
                dve.wait_ge(s_wh, BASE + 2)
                dve.tensor_tensor(bb[32:33], bs[32:33], bb[32:33].bitcast(F32), ALU.subtract).then_inc(s_wl, 1)

                def scale_attn(t, r):
                    dve.wait_ge(s_la[r], BASE + 16 * half_count(t, r))
                    dve.wait_ge(s_i, BASE + t + 1)
                    dve.wait_ge(s_al, BASE + t)
                    dve.tensor_tensor(an[:], at[:, r], ps_i[:], ALU.mult).then_inc(s_an, 1)

                def split_x(t, r):
                    dve.wait_ge(s_xh, BASE + t + 1)
                    dve.tensor_tensor(xl[:, r], ps_x[:], xh[:, r].bitcast(F32), ALU.subtract).then_inc(s_xl, 1)

                def route(t):
                    pair = t // 2
                    dve.wait_ge(s_th, BASE + t + 2)
                    dve.tensor_scalar(sc[:], th[:], 0.5, 0.5, ALU.mult, ALU.add).then_inc(s_sc, 1)
                    dve.wait_ge(s_sc, BASE + pair + 1)
                    dve.tensor_tensor(sel[:], sc[:], eb[:], ALU.add).then_inc(s_sel, 1)
                    dve.wait_ge(s_sel, BASE + pair + 1)
                    dve.memset(spare[:], 0.0)
                    for s in range(PAIR):
                        last = dve.max(top[:, s], sel[:, s])
                    last.then_inc(s_top, 1)
                    dve.wait_ge(s_top, BASE + pair + 1)
                    dve.memset(spare[:], 0.0)
                    for s in range(PAIR):
                        last = dve.match_replace(rest[:, s], top[:, s], sel[:, s], -1e30)
                    last.then_inc(s_rest, 1)
                    dve.wait_ge(s_rest, BASE + pair + 1)
                    dve.tensor_tensor(pick[:], rest[:], sel[:], ALU.not_equal).then_inc(s_pick, 1)
                    dve.wait_ge(s_pick, BASE + pair + 1)
                    dve.tensor_tensor(part[:], pick[:], sc[:], ALU.mult).then_inc(s_part, 1)
                    dve.wait_ge(s_part, BASE + pair + 1)
                    dve.tensor_reduce(tot[:], part[:], AX.X, ALU.add).then_inc(s_tot, 1)
                    dve.wait_ge(s_tot, BASE + pair + 1)
                    dve.reciprocal(inv[:], tot[:]).then_inc(s_ti, 1)
                    dve.wait_ge(s_ti, BASE + pair + 1)
                    dve.scalar_tensor_tensor(combine[:, bass.ds(t * SUB, PAIR), :], part[:], ROUTE_SCALE,
                                             inv[:].rearrange("p (s o) -> p s o", o=1).broadcast_to((P, PAIR, NE)),
                                             ALU.mult, ALU.mult).then_inc(s_c, 1)

                def step(t, r):
                    if there(t + 3):
                        scale_attn(t + 3, 1 - r)
                    if there(t + 1):
                        dve.wait_ge(s_z, BASE + t + 2)
                        z_norm.moments(dve, t + 1, lambda s: ps_z[:, s])
                    if there(t):
                        dve.wait_ge(s_x1, BASE + t + 1)
                        x_norm.moments(dve, t, lambda s: x1[:, r, s])
                    if there(t - 1):
                        if there(t - 3):
                            dve.wait_ge(s_sT[1 - r], BASE + 32 * half_count(t - 3, 1 - r))
                            dve.wait_ge(s_r, BASE + t - 2)
                        split_x(t - 1, 1 - r)
                    if there(t + 3):
                        dve.wait_ge(s_ah, BASE + t + 4)
                        dve.tensor_tensor(al[:, 1 - r], an[:], ah[:, 1 - r].bitcast(F32), ALU.subtract).then_inc(s_al, 1)
                    if r == 1 and there(t - 3):
                        route(t - 3)

                steps(dve, step)

            @block.scalar
            def _(act):
                act.wait_ge(s_sp, BASE + 16)
                act.activation(spread[:], ss[:], ACT.Copy).then_inc(s_spread, 1)
                act.wait_ge(s_w, BASE + 64)
                act.activation(wh[:], ws[:], ACT.Copy).then_inc(s_wh, 1)
                act.wait_ge(s_b, BASE + 32)
                act.activation(bb[:], bs[:], ACT.Copy).then_inc(s_wh, 1)

                def step(t, r):
                    if there(t - 2):
                        act.wait_ge(s_r, BASE + t - 1)
                        if r == 0:
                            act.wait_ge(s_sc, BASE + (t - 2) // 2)
                        act.activation(th[:, r * SUB:(r + 1) * SUB], ps_r[:], ACT.Tanh, scale=0.5).then_inc(s_th, 1)
                    if there(t + 3):
                        act.wait_ge(s_an, BASE + t + 4)
                        act.wait_ge(s_z, BASE + t + 2)
                        act.activation(ah[:, 1 - r], an[:], ACT.Copy).then_inc(s_ah, 1)
                    if there(t + 1):
                        act.wait_ge(s_x1, BASE + t + 1)
                        z_norm.apply(act, t + 1, lambda s: ps_z[:, s], lambda s: zn[:, s])
                    if there(t):
                        act.wait_ge(s_xT, BASE + t)
                        x_norm.apply(act, t, lambda s: x1[:, r, s], lambda s: xn[:, s])
                    if there(t):
                        act.wait_ge(s_xT, BASE + t + 1)
                        if there(t - 2):
                            act.wait_ge(s_sT[r], BASE + 32 * half_count(t - 2, r))
                        act.activation(xh[:, r], ps_x[:], ACT.Copy).then_inc(s_xh, 1)

                steps(act, step)

            @block.tensor
            def _(pe):
                pe.wait_ge(s_inv, BASE + 6)
                pe.wait_ge(s_spread, BASE + 1)

                def spread_inverses(t, half):
                    pe.wait_ge(s_an, BASE + t)
                    for c in range(KC):
                        for n in range(3):
                            last = pe.matmul(ps_i[:, c], spread[:, bass.ds(t - half + c, 1)].rearrange("p o m -> p (o m)"),
                                             dp[:, n, half * TILE:(half + 1) * TILE], start=n == 0, stop=n == 2)
                    last.then_inc(s_i, 1)

                def project(t, r):
                    pe.wait_ge(s_al, BASE + t + 1)
                    pe.wait_ge(z_norm.done, BASE + t)
                    for s in range(SUB):
                        tok = slice(s * P, (s + 1) * P)
                        pe.matmul(ps_z[:, s], ones[:], bb[:], start=True, stop=False)
                        for c in range(KC):
                            a_hi, a_lo = ah[:, r, c, tok], al[:, r, c, tok]
                            w_hi, w_lo = wh[:, c, 0:D], wl[:, c, 0:D]
                            pe.matmul(ps_z[:, s], a_hi, w_hi, start=False, stop=False)
                            pe.matmul(ps_z[:, s], a_hi, w_lo, start=False, stop=False)
                            last = pe.matmul(ps_z[:, s], a_lo, w_hi, start=False, stop=c == KC - 1)
                    last.then_inc(s_z, 1)

                def transposes(t):
                    pe.wait_ge(x_norm.done, BASE + t + 1)
                    pe.wait_ge(s_xl, BASE + t)
                    for c in range(KC):
                        for s in range(SUB):
                            last = pe.transpose(ps_x[:, c, s * P:(s + 1) * P], xn[:, s, c * P:(c + 1) * P], ident[:])
                    last.then_inc(s_xT, 1)

                def router(t, r):
                    pe.wait_ge(s_xl, BASE + t + 1)
                    pe.wait_ge(s_th, BASE + t)
                    for s in range(SUB):
                        tok = slice(s * P, (s + 1) * P)
                        last = three_products(pe, ps_r[:, s], lambda c: xh[:, r, c, tok], lambda c: xl[:, r, c, tok],
                                              lambda c: wh[:, c, D:D + NE], lambda c: wl[:, c, D:D + NE], KC)
                    last.then_inc(s_r, 1)

                def step(t, r):
                    if there(t - 2):
                        router(t - 2, r)
                    if there(t + 4):
                        spread_inverses(t + 4, r)
                    if there(t + 2):
                        if isinstance(t, int) and t + 2 == 0:
                            pe.wait_ge(s_wl, BASE + 3)
                        project(t + 2, r)
                    if there(t):
                        transposes(t)

                steps(pe, step)


def experts(nc, outer, w_exp, w_sh, x1_dram, xT_dram, combine, out):
    with ExitStack() as inner:
        m = Mem(nc, outer, inner, "D")
        one = m.sb("one", [P, 1])
        ws = m.sb("w_stage", [P, 2, 3, KC, D])
        wh = m.sb("w_hi", [P, 2, 3, KC, D], F32R)
        wl = m.sb("w_lo", [P, 2, 3, KC, D], F32R)
        xh = m.sb("xT_hi", [P, GT, KC, TILE], F32R)
        xl = m.sb("xT_lo", [P, GT, KC, TILE], F32R)
        x1 = m.sb("x1", [P, GT, SUB, D])
        y = m.sb("y", [P, GT, SUB, D])
        yn = m.sb("y_normed", [P, SUB, D])
        ob = m.sb("out", [P, 2, SUB, D])
        th = m.sb("tanh", [P, KC, TILE])
        v = m.sb("gated", [P, KC, TILE])
        h = m.sb("hidden", [P, 2, KC, TILE])
        hh = m.sb("hidden_hi", [P, 2, KC, TILE], F32R)
        hl = m.sb("hidden_lo", [P, 2, KC, TILE], F32R)
        ps_g = m.ps("ps_gate", [P, KC, TILE])
        ps_u = m.ps("ps_up", [P, KC, TILE])
        ps_y = m.ps("ps_y", [P, 2, SUB, D])

        NW = NE + 1
        s_ws = [m.sem(f"w_loaded{i}", lifted=False) for i in range(2)]
        s_wh, s_wl, s_one = m.sem("w_hi"), m.sem("w_split"), m.sem("one")
        norm = Norm(m, "norm_y")
        s_x = [m.sem(f"xT_loaded{i}") for i in range(GT)]
        s_x1 = [m.sem(f"x1_loaded{i}") for i in range(GT)]
        s_gu, s_th, s_v, s_h, s_hh, s_hl = (m.sem(n) for n in (
            "hidden_products", "tanh", "gated", "hidden", "hidden_hi", "hidden_split"))
        s_yp, s_acc, s_ob = m.sem("y_products"), m.sem("accumulated"), m.sem("out_done")
        s_st = [m.sem(f"out_stored{i}") for i in range(2)]

        with nc.Block() as block:

            @block.sync
            def _(sp):
                def load_x1(g, tt):
                    sp.dma_start(x1[:, tt], x1_dram[bass.ds(g * GT + tt, 1)].rearrange("o p s d -> p (o s) d")
                                 ).then_inc(s_x1[tt], 16)

                for tt in range(GT):
                    load_x1(0, tt)

                def step(g, more):
                    for tt in range(GT):
                        sp.wait_ge(s_ob, BASE + g * GT + tt + 1)
                        sp.dma_start(out[bass.ds((g * GT + tt) * TILE, TILE), :].rearrange("(s p) d -> p s d", p=P),
                                     ob[:, tt % 2]).then_inc(s_st[tt % 2], 16)
                        if more:
                            load_x1(g + 1, tt)

                with sp.Fori(0, NGR - 1) as g:
                    step(g, True)
                step(NGR - 1, False)
                for i in range(2):
                    sp.wait_ge(s_st[i], BASE + 16 * NT // 2)

            @block.gpsimd
            def _(pool):
                def load(e, r):
                    src = w_sh if e is None else w_exp[bass.ds(e, 1)].rearrange("o p a c n -> p (o a) c n")
                    pool.dma_start(ws[:, r], src).then_inc(s_ws[r], 16)

                def split(w, r, first):
                    pool.wait_ge(s_ws[r], 16 * ((w - r) // 2 + 1))
                    if not first:
                        pool.wait_ge(s_yp, BASE + GT * (w - 1))
                    for a in range(3):
                        pool.tensor_tensor(wh[:, r, a].rearrange("p c n -> p (c n)"),
                                           ws[:, r, a].rearrange("p c n -> p (c n)"),
                                           one[:].broadcast_to((P, KC * D)), ALU.mult).then_inc(s_wh, 1)
                        pool.wait_ge(s_wh, BASE + 3 * w + a + 1)
                        pool.tensor_tensor(wl[:, r, a], ws[:, r, a], wh[:, r, a].bitcast(F32), ALU.subtract
                                           ).then_inc(s_wl, 1)
                    pool.wait_ge(s_wl, BASE + 3 * w + 3)

                def roots(g):
                    for tt in range(GT):
                        norm.root(pool, g * GT + tt)

                load(None, 0)
                load(0, 1)
                m.lift(pool)
                norm.constants(pool)
                pool.memset(one[:], 1.0).then_inc(s_one, 1)
                pool.wait_ge(s_one, BASE + 1)
                for g in range(NGR):
                    w = g * NW
                    split(w, w % 2, w < 2)
                    load(1, w % 2)
                    if g > 0:
                        roots(g - 1)
                    split(w + 1, (w + 1) % 2, w + 1 < 2)
                    load(2, (w + 1) % 2)
                    with pool.Fori(0, (NE - 4) // 2) as it:
                        for k in range(2):
                            r = (w + 2 + k) % 2
                            split(it * 2 + (w + 2 + k), r, False)
                            load(it * 2 + (3 + k), r)
                    for e in range(NE - 3, NE):
                        r = (w + 1 + e) % 2
                        split(w + 1 + e, r, False)
                        if e + 2 < NE:
                            load(e + 2, r)
                        elif g + 1 < NGR:
                            load(None if e + 2 == NE else 0, r)
                roots(NGR - 1)

            @block.vector
            def _(dve):

                def gate(n, tt):
                    r = tt % 2
                    for k in range(KC):
                        dve.wait_ge(s_th, BASE + KC * n + k + 1)
                        dve.scalar_tensor_tensor(v[:, k], th[:, k], 1.0, ps_g[:, k], ALU.add, ALU.mult).then_inc(s_v, 1)
                        dve.wait_ge(s_v, BASE + KC * n + k + 1)
                        dve.scalar_tensor_tensor(h[:, r, k], v[:, k], 0.5, ps_u[:, k], ALU.mult, ALU.mult
                                                 ).then_inc(s_h, 1)

                def low(n, tt):
                    r = tt % 2
                    for k in range(KC):
                        dve.wait_ge(s_hh, BASE + KC * n + k + 1)
                        dve.tensor_tensor(hl[:, r, k], h[:, r, k], hh[:, r, k].bitcast(F32), ALU.subtract
                                          ).then_inc(s_hl, 1)

                def accumulate(n, g, e, tt):
                    dve.wait_ge(s_yp, BASE + n + 1)
                    if e is None:
                        last = dve.tensor_copy(y[:, tt], ps_y[:, tt % 2])
                    else:
                        dve.wait_ge(s_acc, BASE + n - GT + 1)
                        for s in range(SUB):
                            c = combine[:, bass.ds((g * GT + tt) * SUB + s, 1), bass.ds(e, 1)].rearrange(
                                "p a b -> p (a b)")
                            last = dve.scalar_tensor_tensor(y[:, tt, s], ps_y[:, tt % 2, s], c, y[:, tt, s],
                                                            ALU.mult, ALU.add)
                    last.then_inc(s_acc, 1)

                def finish(g, tt):
                    t = g * GT + tt
                    dve.wait_ge(s_acc, BASE + (g * NW + NE) * GT + tt + 1)
                    norm.moments(dve, t, lambda s: y[:, tt, s])
                    norm.apply(dve, t, lambda s: y[:, tt, s], lambda s: yn[:, s])
                    dve.wait_ge(norm.done, BASE + t + 1)
                    dve.wait_ge(s_x1[tt], BASE + 16 * (g + 1))
                    dve.wait_ge(s_st[tt % 2], BASE + 16 * (g * 2 + tt // 2))
                    dve.tensor_tensor(ob[:, tt % 2], x1[:, tt], yn[:], ALU.add).then_inc(s_ob, 1)

                def ahead(n, tt, more=True):
                    if more:
                        gate(n + 1, (tt + 1) % GT)
                        low(n + 1, (tt + 1) % GT)

                def group(g, more):
                    for tt in range(GT):
                        n = g * (NW * GT) + tt
                        ahead(n, tt)
                        accumulate(n, g, None, tt)
                    with dve.Fori(0, NE - 1) as e:
                        for tt in range(GT):
                            n = g * (NW * GT) + (e + 1) * GT + tt
                            ahead(n, tt)
                            accumulate(n, g, e, tt)
                    for tt in range(GT):
                        n = g * (NW * GT) + NE * GT + tt
                        ahead(n, tt, more or tt < GT - 1)
                        accumulate(n, g, NE - 1, tt)
                        finish(g, tt)

                gate(0, 0)
                low(0, 0)
                with dve.Fori(0, NGR - 1) as g:
                    group(g, True)
                group(NGR - 1, False)

            @block.scalar
            def _(act):
                def load_x(g, tt):
                    for hl_, dst in enumerate((xh, xl)):
                        act.dma_start(dst[:, tt].bitcast(F32), xT_dram[bass.ds(g * GT + tt, 1), hl_].rearrange(
                            "o p c n -> p (o c) n")).then_inc(s_x[tt], 16)

                def tanh_and_hi(n, tt):
                    for k in range(KC):
                        act.wait_ge(s_gu, BASE + KC * n + k + 1)
                        act.wait_ge(s_v, BASE + KC * n)
                        act.activation(th[:, k], ps_g[:, k], ACT.Tanh, scale=0.5).then_inc(s_th, 1)
                    for k in range(KC):
                        act.wait_ge(s_h, BASE + KC * n + k + 1)
                        act.activation(hh[:, tt % 2, k], h[:, tt % 2, k], ACT.Copy).then_inc(s_hh, 1)

                for tt in range(GT):
                    load_x(0, tt)

                def group(g, more):
                    first = g * (NW * GT) + 1
                    with act.Fori(0, NE) as e:
                        for tt in range(GT):
                            tanh_and_hi(first + e * GT + tt, (tt + 1) % GT)
                    for tt in range(GT):
                        if more or tt < GT - 1:
                            tanh_and_hi(first + NE * GT + tt, (tt + 1) % GT)
                        if more:
                            load_x(g + 1, tt)

                tanh_and_hi(0, 0)
                with act.Fori(0, NGR - 1) as g:
                    group(g, True)
                group(NGR - 1, False)

            @block.tensor
            def _(pe):
                def hidden(n, w, r, tt):
                    if tt == 0:
                        pe.wait_ge(s_wl, BASE + 3 * w + 3)
                    pe.wait_ge(s_x[tt], BASE + 32 * (w // NW + 1))
                    pe.wait_ge(s_h, BASE + KC * n)
                    for k in range(KC):
                        cols = slice(k * P, (k + 1) * P)
                        for a, o in ((0, ps_g), (1, ps_u)):
                            last = three_products(pe, o[:, k], lambda c: wh[:, r, a, c, cols],
                                                  lambda c: wl[:, r, a, c, cols], lambda c: xh[:, tt, c],
                                                  lambda c: xl[:, tt, c], KC)
                        last.then_inc(s_gu, 1)

                def down(n, r, tt):
                    pe.wait_ge(s_hl, BASE + KC * n + KC)
                    if tt >= 2:
                        pe.wait_ge(s_acc, BASE + n - 1)
                    else:
                        pe.wait_ge(s_acc, BASE + n - tt)
                    b = tt % 2
                    for s in range(SUB):
                        tok = slice(s * P, (s + 1) * P)
                        last = three_products(pe, ps_y[:, b, s], lambda c: hh[:, b, c, tok], lambda c: hl[:, b, c, tok],
                                              lambda c: wh[:, r, 2, c], lambda c: wl[:, r, 2, c], KC)
                    last.then_inc(s_yp, 1)

                def expert(w, r, more):
                    for tt in range(GT):
                        n = w * GT + tt
                        if tt < GT - 1:
                            hidden(n + 1, w, r, tt + 1)
                        elif more:
                            hidden(n + 1, w + 1, 1 - r, 0)
                        down(n, r, tt)

                hidden(0, 0, 0, 0)
                with pe.Fori(0, NGR * NW // 2 - 1) as it:
                    for r in range(2):
                        expert(it * 2 + r, r, True)
                expert(NGR * NW - 2, 0, True)
                expert(NGR * NW - 1, 1, False)


def build(nc, x, w1, b1c, b1v, w2, b2, gate, ebias, w_exp, w_sh, ident, mask, maskT, spread, out):
    qk = nc.dram_tensor("qk_scratch", (2, 2, B * D, S), F32, kind="Internal").ap()
    v = nc.dram_tensor("v_scratch", (NG, NBLK, P, HG * SLOT), F32, kind="Internal").ap()
    attn = nc.dram_tensor("attn_scratch", (B * D, S), F32, kind="Internal").ap()
    den = nc.dram_tensor("den_scratch", (B * H, S), F32, kind="Internal").ap()
    x1 = nc.dram_tensor("x1_scratch", (NT, P, SUB, D), F32, kind="Internal").ap()
    xT = nc.dram_tensor("xT_scratch", (NT, 2, P, KC, TILE), F32, kind="Internal").ap()
    with ExitStack() as outer:
        combine = outer.enter_context(nc.sbuf_tensor("combine", [P, NT * SUB, NE], F32))
        project_qkv(nc, outer, x, w1, b1c, b1v, ident, qk, v)
        attention(nc, outer, ident, ident, mask, maskT, qk, v, attn, den)
        output_and_route(nc, outer, x, w2, b2, gate, ebias, ident, spread, attn, den, x1, xT, combine)
        experts(nc, outer, w_exp, w_sh, x1, xT, combine, out)


def kernel(L0_attn_x, L0_attn_W1, L0_attn_b1, L0_attn_W2, L0_attn_b2, L0_ffn_gate_w, L0_ffn_expert_bias,
           L0_ffn_w_gate, L0_ffn_w_up, L0_ffn_w_down, L0_ffn_shared_gate_w, L0_ffn_shared_up_w,
           L0_ffn_shared_down_w):
    import concourse.bacc as bacc
    from concourse.bass_utils import run_bass_kernel_spmd

    def rows(a):
        return np.broadcast_to(np.asarray(a)[None, :], (P, a.shape[-1]))

    def apart(a):
        return a.reshape(*a.shape[:-2], KC, P, a.shape[-1]).swapaxes(-3, -2)

    def weights(g, u, d):
        return np.stack([apart(np.swapaxes(w, -1, -2)) for w in map(np.asarray, (g, u, d))], axis=-4).swapaxes(-4, -3)

    w1 = np.asarray(L0_attn_W1).reshape(D, H, 3, DH).transpose(0, 2, 1, 3).reshape(D, 3 * D)
    b1 = np.asarray(L0_attn_b1).reshape(H, 3, DH).transpose(1, 0, 2).reshape(3 * D)
    i = np.arange(P)
    arrays = {
        "x": np.asarray(L0_attn_x).reshape(T, D), "w1": w1, "b1c": b1[:2 * D].reshape(4, P).T, "b1v": rows(b1[2 * D:]),
        "w2": np.asarray(L0_attn_W2), "b2": rows(L0_attn_b2), "gate": np.asarray(L0_ffn_gate_w).T,
        "ebias": rows(np.tile(np.asarray(L0_ffn_expert_bias), 2 * SUB)), "w_exp": weights(L0_ffn_w_gate, L0_ffn_w_up, L0_ffn_w_down),
        "w_sh": weights(L0_ffn_shared_gate_w, L0_ffn_shared_up_w, L0_ffn_shared_down_w),
        "ident": np.eye(P, dtype=np.float32),
        "mask": np.where(i[None, :] > i[:, None], MASK, 0.0).astype(np.float32),
        "maskT": np.where(i[None, :] < i[:, None], MASK, 0.0).astype(np.float32),
        "spread": np.repeat(np.eye(P, dtype=np.float32), DH, axis=1),
    }
    arrays = {f"in_{k}": np.ascontiguousarray(a) for k, a in arrays.items()}
    nc = bacc.Bacc("TRN2", target_bir_lowering=False, num_devices=1)
    aps = [nc.dram_tensor(k, a.shape, mybir.dt.from_np(a.dtype), kind="ExternalInput").ap() for k, a in arrays.items()]
    out = nc.dram_tensor("out", (T, D), F32, kind="ExternalOutput").ap()
    build(nc, *aps, out)
    got = run_bass_kernel_spmd(nc, [arrays], core_ids=[0]).results[0]["out"]
    return got.reshape(B, S, D)
```

```python
from contextlib import ExitStack

import numpy as np

import concourse.bass as bass
from concourse import mybir

ALU = mybir.AluOpType
ACT = mybir.ActivationFunctionType
AX = mybir.AxisListType
F32 = mybir.dt.float32
F32R = mybir.dt.float32r
BF16 = mybir.dt.bfloat16

P = 128
EPS = 1e-5
B, S, D, H, DH = 8, 1024, 256, 16, 16
T = B * S
TILE = 512
NT = T // TILE
SUB = TILE // P
KC = D // P
HG = 4
NGH = H // HG
NG = B * NGH
SLOT = 32
NBLK = S // P
NE, TOPK, F = 16, 8, 256
ROUTE_SCALE = 2.826
MASK = -4e10
GT = 4
BASE = 1
NGR = NT // GT


class Mem:

    def __init__(self, nc, outer, inner, stage):
        self.nc, self.outer, self.inner, self.stage = nc, outer, inner, stage
        self.sems = []

    def sb(self, name, shape, dt=F32):
        return self.inner.enter_context(self.nc.sbuf_tensor(f"{self.stage}_{name}", shape, dt))

    def ps(self, name, shape, dt=F32):
        return self.inner.enter_context(self.nc.psum_tensor(f"{self.stage}_{name}", shape, dt))

    def sem(self, name, lifted=True):
        s = self.outer.enter_context(self.nc.semaphore(f"{self.stage}_{name}"))
        if lifted:
            self.sems.append(s)
        return s

    def lift(self, eng):
        for s in self.sems:
            eng.sem_inc(s, BASE)


def three_products(pe, out, lhs_hi, lhs_lo, rhs_hi, rhs_lo, chunks):
    pairs = [(lhs_hi, rhs_hi), (lhs_hi, rhs_lo), (lhs_lo, rhs_hi)]
    last = None
    for c in range(chunks):
        for n, (a, b) in enumerate(pairs):
            last = pe.matmul(out, a(c), b(c), start=(c == 0 and n == 0), stop=(c == chunks - 1 and n == 2))
    return last


class Norm:

    def __init__(self, m, name, lead=0):
        self.lead = lead
        self.spare = m.sb(f"{name}_spare", [P, 1])
        self.const = m.sb(f"{name}_const", [P, 3])
        self.st = m.sb(f"{name}_stats", [P, SUB, 6])
        self.mv = m.sb(f"{name}_meanvar", [P, SUB, 2])
        self.ve = m.sb(f"{name}_var_eps", [P, SUB])
        self.nm = m.sb(f"{name}_neg_mean", [P, SUB])
        self.rs = m.sb(f"{name}_rstd", [P, SUB])
        self.sh = m.sb(f"{name}_shift", [P, SUB])
        self.set, self.stats, self.aggr, self.added, self.power, self.shift, self.done = (
            m.sem(f"{name}_{k}") for k in ("set", "stats", "aggr", "added", "power", "shift", "done"))

    def constants(self, pool):
        for n, value in enumerate((EPS, -0.5, -1.0)):
            pool.memset(self.const[:, n:n + 1], value).then_inc(self.set, 1)
        pool.wait_ge(self.set, BASE + 3)

    def root(self, pool, t):
        pool.wait_ge(self.aggr, BASE + t + 1)
        pool.tensor_tensor(self.ve[:], self.mv[:, :, 1], self.const[:, 0:1].broadcast_to((P, SUB)), ALU.add
                           ).then_inc(self.added, 1)
        pool.tensor_tensor(self.nm[:], self.mv[:, :, 0], self.const[:, 2:3].broadcast_to((P, SUB)), ALU.mult
                           ).then_inc(self.added, 1)
        pool.wait_ge(self.added, BASE + 2 * t + 2)
        pool.wait_ge(self.done, BASE + self.lead + t)
        pool.tensor_tensor(self.rs[:], self.ve[:], self.const[:, 1:2].broadcast_to((P, SUB)), ALU.pow
                           ).then_inc(self.power, 1)
        pool.wait_ge(self.power, BASE + t + 1)
        pool.tensor_tensor(self.sh[:], self.nm[:], self.rs[:], ALU.mult).then_inc(self.shift, 1)

    def moments(self, dve, t, src):
        for s in range(SUB):
            last = dve.bn_stats(self.st[:, s], src(s))
        last.then_inc(self.stats, 1)
        dve.wait_ge(self.stats, BASE + t + 1)
        dve.wait_ge(self.added, BASE + 2 * t)
        dve.memset(self.spare[:], 0.0)
        for s in range(SUB):
            last = dve.bn_aggr(self.mv[:, s], self.st[:, s])
        last.then_inc(self.aggr, 1)

    def apply(self, act, t, src, dst):
        act.wait_ge(self.shift, BASE + t + 1)
        for s in range(SUB):
            last = act.activation(dst(s), src(s), ACT.Identity, bias=self.sh[:, s:s + 1], scale=self.rs[:, s:s + 1])
        last.then_inc(self.done, 1)


def half_count(t, r):
    return (t + 2 - r) // 2


def pipelined(eng, step):
    with eng.Fori(0, NT // 2 - 1) as it:
        for r in range(2):
            step(it * 2 + r, r, True)
    step(NT - 2, 0, True)
    step(NT - 1, 1, False)


def project_qkv(nc, outer, x, w1, b1c, b1v, ident_in, qk_dram, v_dram):
    with ExitStack() as inner:
        m = Mem(nc, outer, inner, "A")
        xt = m.sb("x", [P, 2, SUB, D])
        xn = m.sb("xn", [P, SUB, D])
        ident = m.sb("ident", [P, P])
        ws = m.sb("w_stage", [P, KC, 3 * D])
        wh = m.sb("w_hi", [P, KC, 3 * D], F32R)
        wl = m.sb("w_lo", [P, KC, 3 * D], F32R)
        bc = m.sb("bias_qk", [P, 4])
        bv = m.sb("bias_v", [P, D])
        xh = m.sb("xT_hi", [P, 2, KC, TILE], F32R)
        xl = m.sb("xT_lo", [P, 2, KC, TILE], F32R)
        qh = m.sb("qk_hi", [P, 2, 4, TILE], F32R)
        ql = m.sb("qk_lo", [P, 2, 4, TILE], F32R)
        vt = m.sb("v", [P, 2, SUB, D])
        ps_x = m.ps("ps_xT", [P, KC, TILE])
        ps_q = m.ps("ps_qk", [P, 4, TILE])
        ps_v = m.ps("ps_v", [P, 2, 2, D])

        s_i = m.sem("ident_loaded")
        s_w, s_wh, s_wsplit = m.sem("weights_loaded"), m.sem("w_hi"), m.sem("w_split")
        s_x = [m.sem(f"x_loaded{i}") for i in range(2)]
        norm = Norm(m, "norm")
        s_xT, s_xh, s_xl = m.sem("transposed"), m.sem("xT_hi_done"), m.sem("xT_split")
        s_q, s_qh, s_ql = m.sem("qk_product"), m.sem("qk_hi_done"), m.sem("qk_split")
        s_v, s_vc = m.sem("v_product"), m.sem("v_copied")
        s_st = [m.sem(f"stored{i}") for i in range(2)]
        STORES = 4 * 2 + 1

        with nc.Block() as block:

            @block.sync
            def _(sp):
                sp.dma_start(xt[:, 0], x[0:TILE, :].rearrange("(s p) d -> p s d", p=P)).then_inc(s_x[0], 16)
                sp.dma_start(ident[:], ident_in).then_inc(s_i, 16)
                sp.dma_start(ws[:], w1.rearrange("(c p) f -> p c f", p=P)).then_inc(s_w, 16)
                sp.dma_start(bc[:], b1c).then_inc(s_w, 16)
                sp.dma_start(bv[:], b1v).then_inc(s_w, 16)
                sp.dma_start(xt[:, 1], x[TILE:2 * TILE, :].rearrange("(s p) d -> p s d", p=P)).then_inc(s_x[1], 16)

                def step(t, r, more):
                    if more:
                        sp.wait_ge(norm.done, BASE + t + 1)
                        sp.dma_start(xt[:, r], x[bass.ds((t + 2) * TILE, TILE), :].rearrange(
                            "(s p) d -> p s d", p=P)).then_inc(s_x[r], 16)
                    b_, half = t // 2, r
                    for c in range(4):
                        sp.wait_ge(s_ql, BASE + 4 * t + c + 1)
                        for hl, src in enumerate((qh, ql)):
                            sp.dma_start(qk_dram[c // 2, hl, bass.ds(b_ * D + (c % 2) * P, P),
                                                 half * TILE:(half + 1) * TILE], src[:, r, c].bitcast(F32)).then_inc(s_st[r], 16)
                    sp.wait_ge(s_vc, BASE + 2 * t + 2)
                    sp.dma_start(v_dram[bass.ds(t * TILE, TILE), :].rearrange("(s p) d -> p s d", p=P),
                                 vt[:, r]).then_inc(s_st[r], 16)

                with sp.Fori(0, NT // 2 - 1) as it:
                    for r in range(2):
                        step(it * 2 + r, r, True)
                step(NT - 2, 0, False)
                step(NT - 1, 1, False)
                for r in range(2):
                    sp.wait_ge(s_st[r], BASE + 16 * STORES * NT // 2)

            @block.gpsimd
            def _(pool):
                m.lift(pool)
                norm.constants(pool)
                norm.root(pool, 0)
                pipelined(pool, lambda t, r, more: norm.root(pool, t + 1) if more else None)

            @block.vector
            def _(dve):

                def front(t, r):
                    dve.wait_ge(s_x[r], BASE + (t // 2 + 1) * 16)
                    norm.moments(dve, t, lambda s: xt[:, r, s])

                def split(t, r):
                    dve.wait_ge(s_xh, BASE + t + 1)
                    dve.tensor_tensor(xl[:, r], ps_x[:], xh[:, r].bitcast(F32), ALU.subtract).then_inc(s_xl, 1)

                def step(t, r, more):
                    for c in range(4):
                        dve.wait_ge(s_qh, BASE + 4 * t + c + 1)
                        dve.scalar_tensor_tensor(ql[:, r, c], ps_q[:, c], bc[:, c:c + 1], qh[:, r, c].bitcast(F32),
                                                 ALU.add, ALU.subtract).then_inc(s_ql, 1)
                    if more:
                        split(t + 1, 1 - r)
                    if not isinstance(t, int):
                        front(t + 2, r)
                    dve.wait_ge(s_st[r], BASE + (t // 2) * 16 * STORES)
                    for k in range(2):
                        dve.wait_ge(s_v, BASE + 2 * t + k + 1)
                        for j in range(2):
                            s = 2 * k + j
                            last = dve.tensor_tensor(vt[:, r, s], ps_v[:, k, j], bv[:], ALU.add)
                        last.then_inc(s_vc, 1)

                front(0, 0)
                split(0, 0)
                dve.wait_ge(s_w, BASE + 48)
                dve.wait_ge(s_wh, BASE + 1)
                dve.tensor_tensor(wl[:], ws[:], wh[:].bitcast(F32), ALU.subtract).then_inc(s_wsplit, 1)
                front(1, 1)
                pipelined(dve, step)

            @block.scalar
            def _(act):

                def normed(t, r):
                    act.wait_ge(s_xT, BASE + t)
                    norm.apply(act, t, lambda s: xt[:, r, s], lambda s: xn[:, s])

                def split(t, r):
                    act.wait_ge(s_xT, BASE + t + 1)
                    act.activation(xh[:, r], ps_x[:], ACT.Copy).then_inc(s_xh, 1)

                def step(t, r, more):
                    act.wait_ge(s_st[r], BASE + (t // 2) * 16 * STORES)
                    for c in range(4):
                        act.wait_ge(s_q, BASE + 4 * t + c + 1)
                        act.activation(qh[:, r, c], ps_q[:, c], ACT.Identity, bias=bc[:, c:c + 1]).then_inc(s_qh, 1)
                        if more and c == 1:
                            normed(t + 1, 1 - r)
                    if more:
                        split(t + 1, 1 - r)

                normed(0, 0)
                split(0, 0)
                act.wait_ge(s_w, BASE + 48)
                act.activation(wh[:], ws[:], ACT.Copy).then_inc(s_wh, 1)
                pipelined(act, step)

            @block.tensor
            def _(pe):
                pe.wait_ge(s_i, BASE + 16)

                def transposes(t):
                    pe.wait_ge(norm.done, BASE + t + 1)
                    pe.wait_ge(s_xl, BASE + t)
                    for c in range(KC):
                        for s in range(SUB):
                            last = pe.transpose(ps_x[:, c, s * P:(s + 1) * P], xn[:, s, c * P:(c + 1) * P], ident[:])
                    last.then_inc(s_xT, 1)

                def step(t, r, more):
                    pe.wait_ge(s_xl, BASE + t + 1)
                    for c in range(4):
                        pe.wait_ge(s_ql, BASE + 4 * t)
                        three_products(pe, ps_q[:, c], lambda k: wh[:, k, c * P:(c + 1) * P],
                                       lambda k: wl[:, k, c * P:(c + 1) * P], lambda k: xh[:, r, k],
                                       lambda k: xl[:, r, k], KC).then_inc(s_q, 1)
                    if more:
                        transposes(t + 1)
                    for k2 in range(2):
                        pe.wait_ge(s_vc, BASE + 2 * t)
                        for j in range(2):
                            s = 2 * k2 + j
                            last = three_products(pe, ps_v[:, k2, j], lambda k: xh[:, r, k, s * P:(s + 1) * P],
                                                  lambda k: xl[:, r, k, s * P:(s + 1) * P],
                                                  lambda k: wh[:, k, 2 * D:3 * D], lambda k: wl[:, k, 2 * D:3 * D], KC)
                        last.then_inc(s_v, 1)

                transposes(0)
                pe.wait_ge(s_wsplit, BASE + 1)
                pipelined(pe, step)


PAIRS = {i: [(i, (h, h + 1)) for h in (0, 2)] for i in range(4)}
SINGLES = {i: [(i, (h,)) for h in range(HG)] for i in range(4, NBLK)}
UNITS = (SINGLES[6][:2] + SINGLES[5][:2] + PAIRS[1] + SINGLES[4][:2] + SINGLES[5][2:] + PAIRS[2] + PAIRS[0]
         + SINGLES[4][2:] + SINGLES[6][2:] + SINGLES[7] + PAIRS[3])
FIRST = len(UNITS)
KEYS = [(qh, j) for qh in range(2) for j in range(4 * (qh + 1))]
QUADS = len(KEYS)
SLOTS = 3
PAD = 96
SHIFT = PAD + 2
HALF = KEYS.index((1, 0))
EARLY = 10
SPLIT = 384
MAX_AT = 2 + FIRST - EARLY + 1


def width(qh, j):
    return TILE - max(0, j * P - qh * TILE)


def two_heads(ps, slot, w):
    if w <= TILE // 2:
        return ps[:, slot, 0:2 * w].rearrange("p (h n) -> p h n", h=2)
    return ps[:, slot].rearrange("p (h n) -> p h n", h=2)[:, :, 0:w]


def schedule():
    units = []
    for k in range(2 * QUADS):
        units.append(("second", 2 + k))
        if k < FIRST - EARLY:
            units.append(("next", EARLY + k))
        else:
            units.append(("after", k - (FIRST - EARLY)))
    return units


def attention(nc, outer, ident_in, mask_in, maskT_in, qk_dram, v_dram, a_dram, den_dram):
    with ExitStack() as inner:
        m = Mem(nc, outer, inner, "B")
        qs = m.sb("q_stack", [P, 3, HG, S], F32R)
        ks = m.sb("k_stack", [P, 3, HG, S], F32R)
        vr = m.sb("v_raw", [P, 3, NBLK, HG * DH])
        vs = m.sb("v", [P, 3, NBLK, HG, SLOT])
        one = m.sb("one", [P, 1])
        pt = m.sb("probs", [P, SLOTS, HG, TILE])
        mx = m.sb("max", [P, 3, HG, NBLK])
        mh = m.sb("neg_max_hi", [HG * NBLK, P], F32R)
        ml = m.sb("neg_max_lo", [HG * NBLK, P], F32R)
        ident = m.sb("ident", [P, P])
        identr = m.sb("ident_r", [P, P], F32R)
        mask = m.sb("mask", [P, P], F32R)
        maskT = m.sb("maskT", [P, P], F32R)
        on = m.sb("out_raw", [P, 2, TILE])
        stage = m.sb("mask_stage", [P, 3, P])
        ps = m.ps("slots", [P, SLOTS, 2 * TILE])
        po = m.ps("ps_out", [P, TILE])
        pm = m.ps("ps_maxT", [P, TILE])

        s_c, s_set, s_kset = m.sem("constants_loaded"), m.sem("constants_set"), m.sem("k_constants_set")
        s_ld = [m.sem(f"group_loaded{i}") for i in range(3)]
        s_sc1, s_max = m.sem("first_scores"), m.sem("first_max")
        s_mT, s_mh, s_ml, s_row = m.sem("maxT"), m.sem("neg_max_hi"), m.sem("neg_max"), m.sem("max_rows")
        s_sc2, s_exp = m.sem("second_scores"), m.sem("exped")
        s_v = m.sem("v_spread")
        s_pfree = m.sem("probs_free")
        s_on = m.sem("out_raw")
        s_st = [m.sem(f"out_stored{i}") for i in range(2)]
        LOADS, STORES = 7, 16 * 2 * HG
        sched = schedule()

        def in_loop(eng, step):
            with eng.Fori(0, NG // 3) as it:
                for r in range(3):
                    step(it * 3 + r, r, True, True)
            step(NG - 2, 0, True, False)
            step(NG - 1, 1, False, False)

        with nc.Block() as block:

            @block.sync
            def _(sp):
                def load_rows(g, r, rows):
                    for row in rows:
                        hl = (0, 1, 0)[row]
                        sp.dma_start(qs[row * DH:(row + 1) * DH, r].bitcast(F32), qk_dram[
                            0, hl, bass.ds(g * HG * DH, HG * DH), :].rearrange("(h d) n -> d h n", d=DH)
                        ).then_inc(s_ld[r], 16)
                    for row in rows:
                        hl = (0, 0, 1)[row]
                        sp.dma_start(ks[row * DH:(row + 1) * DH, r].bitcast(F32), qk_dram[
                            1, hl, bass.ds(g * HG * DH, HG * DH), :].rearrange("(h d) n -> d h n", d=DH)
                        ).then_inc(s_ld[r], 16)

                def load(g, r, rows=range(3)):
                    load_rows(g, r, rows)
                    sp.dma_start(vr[:, r], v_dram[bass.ds(g // NGH * S, S), bass.ds(g % NGH * (HG * DH), HG * DH)].rearrange(
                        "(j p) f -> p j f", p=P)).then_inc(s_ld[r], 16)

                def max_rows(g, r):
                    sp.wait_ge(s_ml, BASE + g + 1)
                    for row, src in ((PAD, mh), (PAD + 1, ml)):
                        sp.dma_start(qs[row:row + 1, r].bitcast(F32).rearrange("o h (i q) -> o (h i) q", q=P),
                                     src[:].bitcast(F32)).then_inc(s_row, 16)

                def store(g, qh):
                    sp.wait_ge(s_on, BASE + 2 * g + qh + 1)
                    for h in range(HG):
                        sp.dma_start(a_dram[bass.ds(g * HG * DH + h * DH, DH), qh * TILE:(qh + 1) * TILE],
                                     on[h * SLOT:h * SLOT + DH, qh]).then_inc(s_st[qh], 16)
                        sp.dma_start(den_dram[bass.ds(g * HG + h, 1), qh * TILE:(qh + 1) * TILE],
                                     on[h * SLOT + DH:h * SLOT + DH + 1, qh]).then_inc(s_st[qh], 16)

                load(0, 0, (0, 1))
                sp.dma_start(ident[:], ident_in).then_inc(s_c, 16)
                sp.dma_start(stage[:, 0], ident_in).then_inc(s_c, 16)
                sp.dma_start(stage[:, 1], mask_in).then_inc(s_c, 16)
                sp.dma_start(stage[:, 2], maskT_in).then_inc(s_c, 16)
                sp.wait_ge(s_set, BASE + 1)
                sp.wait_ge(s_kset, BASE + 1)
                load_rows(0, 0, (2,))
                sp.wait_ge(s_kset, BASE + 6)
                load(1, 1)
                max_rows(0, 0)
                sp.wait_ge(s_kset, BASE + 11)
                load(2, 2)

                def step(g, r, more, loads):
                    if more:
                        max_rows(g + 1, (r + 1) % 3)
                    store(g, 0)
                    if loads:
                        sp.wait_ge(s_pfree, BASE + SLOTS + (g + 1) * QUADS)
                        load(g + 3, r)
                    store(g, 1)

                with sp.Fori(0, NG // 3 - 1) as it:
                    for r in range(3):
                        step(it * 3 + r, r, True, True)
                for g in range(NG // 3 * 3 - 3, NG):
                    step(g, g % 3, g + 1 < NG, g + 3 < NG)
                for qh in range(2):
                    sp.wait_ge(s_st[qh], BASE + NG * STORES)

            @block.gpsimd
            def _(pool):
                m.lift(pool)

                def spread_v(g, r):
                    pool.wait_ge(s_ld[r], BASE + ((g - r) // 3 + 1) * 16 * LOADS)
                    pool.tensor_tensor(vs[:, r, :, :, 0:DH].rearrange("p j h e -> p (j h) e"),
                                       vr[:, r].rearrange("p j (h e) -> p (j h) e", h=HG),
                                       one[:].rearrange("p (a b) -> p a b", a=1).broadcast_to((P, NBLK * HG, DH)),
                                       ALU.mult).then_inc(s_v, 1)

                sets = [(ks[32:64, 0], 0.0), (ks[64:PAD, 0], 0.0), (ks[PAD:P, 0], 1.0), (qs[:, 1], 0.0), (ks[0:PAD, 1], 0.0), (ks[PAD:P, 1], 1.0),
                        (vs[:], 1.0), (one[:], 1.0), (qs[:, 2], 0.0), (ks[0:PAD, 2], 0.0), (ks[PAD:P, 2], 1.0)]
                for n, (dst, value) in enumerate(sets):
                    if n > 0:
                        pool.wait_ge(s_kset, BASE + n)
                    if n == 8:
                        spread_v(0, 0)
                        pool.wait_ge(s_v, BASE + 1)
                    pool.memset(dst if n in (6, 7) else dst.bitcast(F32), value).then_inc(s_kset, 1)
                pool.wait_ge(s_kset, BASE + len(sets))
                spread_v(1, 1)
                spread_v(2, 2)
                with pool.Fori(0, NG // 3 - 1) as it:
                    for r in range(3):
                        pool.wait_ge(s_pfree, BASE + SLOTS + (it * 3 + (r + 1)) * QUADS)
                        spread_v(it * 3 + (r + 3), r)
                for g in range(NG // 3 * 3, NG):
                    pool.wait_ge(s_pfree, BASE + SLOTS + (g - 2) * QUADS)
                    spread_v(g, g % 3)

            @block.vector
            def _(dve):
                dve.memset(qs[32:64, 0].bitcast(F32), 0.0).then_inc(s_set, 1)
                dve.memset(qs[64:P, 0].bitcast(F32), 0.0).then_inc(s_set, 1)
                dve.wait_ge(s_c, BASE + 64)
                dve.tensor_copy(identr[:], stage[:, 0]).then_inc(s_set, 1)
                dve.tensor_copy(mask[:], stage[:, 1]).then_inc(s_set, 1)
                dve.tensor_copy(maskT[:], stage[:, 2]).then_inc(s_set, 1)

                def maxima(g, r, u, slot):
                    i, heads = UNITS[u]
                    w = (i + 1) * P
                    dve.wait_ge(s_sc1, BASE + g * FIRST + u + 1)
                    if len(heads) == 2:
                        src = two_heads(ps, slot, w)
                    else:
                        src = ps[:, slot, 0:w]
                    dve.tensor_reduce(mx[:, r, heads[0]:heads[-1] + 1, i], src, AX.X, ALU.max).then_inc(s_max, 1)

                def rows(g):
                    dve.wait_ge(s_mT, BASE + g + 1)
                    dve.wait_ge(s_row, BASE + 32 * g)
                    n = HG * NBLK
                    dve.tensor_scalar(mh[:], pm[0:n, 0:P], -1.0, None, ALU.mult).then_inc(s_mh, 1)
                    dve.wait_ge(s_mh, BASE + g + 1)
                    dve.scalar_tensor_tensor(ml[:], pm[0:n, 0:P], -1.0, mh[:].bitcast(F32), ALU.mult,
                                             ALU.subtract).then_inc(s_ml, 1)

                for u in range(FIRST):
                    maxima(0, 0, u, u % SLOTS)
                for u in range(EARLY):
                    maxima(1, 1, u, u % SLOTS)
                    if u == 1:
                        rows(0)

                def step(g, r, next_, after):
                    for n, (kind, u) in enumerate(sched):
                        if kind == "next" and next_:
                            maxima(g + 1, (r + 1) % 3, u, n % SLOTS)
                        if kind == "after" and after:
                            maxima(g + 2, (r + 2) % 3, u, n % SLOTS)
                        if (kind, u) == ("after", 0) and next_:
                            rows(g + 1)

                in_loop(dve, step)

            @block.scalar
            def _(act):
                def exps(g, v, slot):
                    qh, j = KEYS[v // 2 % QUADS]
                    buf = v // 2 % SLOTS
                    w = width(qh, j)
                    act.wait_ge(s_sc2, BASE + g * 2 * QUADS + v + 1)
                    if v % 2 == 0:
                        act.wait_ge(s_pfree, BASE + g * QUADS + v // 2 + 1)
                    h = v % 2 * 2
                    act.activation(pt[:, buf, h:h + 2, 0:w], two_heads(ps, slot, w),
                                   ACT.Exp, scale=float(DH) ** -0.5).then_inc(s_exp, 1)

                def raw(g, qh):
                    act.wait_ge(s_pfree, BASE + SLOTS + g * QUADS + (QUADS if qh else HALF))
                    act.wait_ge(s_st[qh], BASE + g * STORES)
                    act.activation(on[:, qh], po[:], ACT.Copy).then_inc(s_on, 1)

                for v in range(2):
                    exps(0, v, (2 * (v - 2)) % SLOTS)

                def step(g, r, more, after):
                    for n, (kind, v) in enumerate(sched):
                        if kind == "second" and (more or v < 2 * QUADS):
                            exps(g, v, n % SLOTS)
                        if (kind, v) == ("second", 2 * HALF + 1):
                            raw(g, 0)
                    raw(g, 1)

                in_loop(act, step)

            @block.tensor
            def _(pe):
                pe.sem_inc(s_pfree, SLOTS)
                pe.wait_ge(s_set, BASE + 5)
                pe.wait_ge(s_kset, BASE + 2)

                def twice(mask_):
                    return mask_[:].rearrange("p (o n) -> p o n", o=1).broadcast_to((P, 2, P))

                def first(g, r, u, slot):
                    i, heads = UNITS[u]
                    w = (i + 1) * P
                    if w <= TILE // 2:
                        both = two_heads(ps, slot, w)
                        for b, h in enumerate(heads):
                            pe.matmul(both[:, b], qs[0:PAD, r, h, i * P:(i + 1) * P], ks[0:PAD, r, h, 0:w],
                                      start=b == 0, stop=False)
                        pe.matmul(both[:, :, w - P:w], identr[:], twice(mask), start=False, stop=True
                                  ).then_inc(s_sc1, 1)
                        return
                    for b, h in enumerate(heads):
                        o = ps[:, slot, b * TILE:(b + 1) * TILE]
                        q = qs[0:PAD, r, h, i * P:(i + 1) * P]
                        if w > TILE:
                            pe.matmul(o, q, ks[0:PAD, r, h, 0:TILE], start=True, stop=True)
                            o = ps[:, slot, TILE:2 * TILE]
                            pe.matmul(o[:, 0:w - TILE], q, ks[0:PAD, r, h, TILE:w], start=True, stop=False)
                        else:
                            pe.matmul(o[:, 0:w], q, ks[0:PAD, r, h, 0:w], start=True, stop=False)
                        at = (w - P) % TILE
                        last = pe.matmul(o[:, at:at + P], identr[:], mask[:], start=False, stop=True)
                    last.then_inc(s_sc1, 1)

                def second(g, r, v, slot):
                    qh, j = KEYS[v // 2 % QUADS]
                    w = width(qh, j)
                    q0 = (qh + 1) * TILE - w
                    both = two_heads(ps, slot, w)
                    if w <= TILE // 2:
                        for b in range(2):
                            h = v % 2 * 2 + b
                            pe.matmul(both[:, b], ks[0:SHIFT, r, h, j * P:(j + 1) * P],
                                      qs[0:SHIFT, r, h, q0:q0 + w], start=b == 0, stop=False)
                        pe.matmul(both[:, :, 0:P], identr[:], twice(maskT), start=False, stop=True
                                  ).then_inc(s_sc2, 1)
                        return
                    for b in range(2):
                        h = v % 2 * 2 + b
                        o = ps[:, slot, b * TILE:b * TILE + w]
                        diagonal = q0 == j * P
                        last = pe.matmul(o, ks[0:SHIFT, r, h, j * P:(j + 1) * P], qs[0:SHIFT, r, h, q0:q0 + w],
                                         start=True, stop=not diagonal)
                        if diagonal:
                            last = pe.matmul(o[:, 0:P], identr[:], maskT[:], start=False, stop=True)
                    last.then_inc(s_sc2, 1)

                def values(g, r, k, part):
                    qh, j = KEYS[k]
                    w = width(qh, j)
                    cols = [(0, w // 2), (w // 2, w)] if w >= SPLIT else [None, (0, w)]
                    if cols[part] is None:
                        return
                    c0, c1 = cols[part]
                    if c0 == 0:
                        if k == 0:
                            pe.wait_ge(s_v, BASE + g + 1)
                        pe.wait_ge(s_exp, BASE + g * 2 * QUADS + 2 * k + 2)
                        if j == 0:
                            pe.wait_ge(s_on, BASE + 2 * g + qh)
                    for h in range(HG):
                        last = pe.matmul(po[h * SLOT:(h + 1) * SLOT, TILE - w + c0:TILE - w + c1],
                                         vs[:, r, j, h], pt[:, k % SLOTS, h, c0:c1],
                                         start=(j == 0 and c0 == 0), stop=(j == 4 * (qh + 1) - 1))
                    if part == 1:
                        last.then_inc(s_pfree, 1)

                def max_transpose(g, r):
                    pe.wait_ge(s_max, BASE + (g + 1) * FIRST)
                    pe.wait_ge(s_ml, BASE + g)
                    pe.transpose(pm[0:HG * NBLK, 0:P], mx[:, r].rearrange("p h i -> p (h i)"), ident[:]).then_inc(s_mT, 1)

                def group_loaded(g, r):
                    pe.wait_ge(s_ld[r], BASE + ((g - r) // 3 + 1) * 16 * LOADS)

                group_loaded(0, 0)
                for u in range(FIRST):
                    if u >= SLOTS:
                        pe.wait_ge(s_max, BASE + u - SLOTS + 1)
                    first(0, 0, u, u % SLOTS)
                group_loaded(1, 1)
                for u in range(EARLY):
                    pe.wait_ge(s_max, BASE + FIRST + u - SLOTS + 1)
                    first(1, 1, u, u % SLOTS)
                    if u == 1:
                        max_transpose(0, 0)
                pe.wait_ge(s_max, BASE + FIRST + EARLY)
                pe.wait_ge(s_row, BASE + 32)
                pe.wait_ge(s_kset, BASE + 3)
                for v in range(2):
                    second(0, 0, v, (2 * (v - 2)) % SLOTS)

                def slot_free(g, n, next_, after):
                    for p in (n - SLOTS, n - 2 * SLOTS):
                        back = 1 if p < 0 else 0
                        kind, u = sched[p]
                        if kind == "second":
                            pe.wait_ge(s_exp, BASE + (g - back) * 2 * QUADS + u + 1)
                            return
                        if kind == "next" and (next_ or back):
                            pe.wait_ge(s_max, BASE + (g + 1 - back) * FIRST + u + 1)
                            return
                        if kind == "after" and (next_ if back else after):
                            pe.wait_ge(s_max, BASE + (g + 2 - back) * FIRST + u + 1)
                            return

                def step(g, r, next_, after):
                    for n, (kind, u) in enumerate(sched):
                        if kind == "second" and u < 2 * QUADS:
                            slot_free(g, n, next_, after)
                            second(g, r, u, n % SLOTS)
                        elif kind == "second" and next_:
                            slot_free(g, n, next_, after)
                            if u == 2 * QUADS:
                                pe.wait_ge(s_row, BASE + 32 * (g + 2))
                            second(g + 1, (r + 1) % 3, u - 2 * QUADS, n % SLOTS)
                        elif kind == "next" and next_:
                            slot_free(g, n, next_, after)
                            first(g + 1, (r + 1) % 3, u, n % SLOTS)
                        elif kind == "after" and after:
                            if u == 0:
                                group_loaded(g + 2, (r + 2) % 3)
                            slot_free(g, n, next_, after)
                            first(g + 2, (r + 2) % 3, u, n % SLOTS)
                        if next_ and (kind, u) == ("second", MAX_AT):
                            max_transpose(g + 1, (r + 1) % 3)
                        if n % 2 == 1:
                            values(g, r, n // 4, n % 4 // 2)

                in_loop(pe, step)


def output_and_route(nc, outer, x, w2, b2, gate, ebias, ident_in, spread_in, a_dram, den_dram,
                     x1_dram, xT_dram, combine, w_exp, w_sh, weights, tiles):
    ews, ewh, ewl, s_ews = weights
    exh, exl, s_ex = tiles
    AHEAD, LAG = 4, 2
    PAIR = 2 * SUB
    with ExitStack() as inner:
        m = Mem(nc, outer, inner, "C")
        at = m.sb("attnT", [P, 2, KC, TILE])
        den = m.sb("denominators", [P, S])
        dp = m.sb("inverse_parts", [P, 3, S], BF16)
        rem = m.sb("inverse_rest", [P, S])
        spread = m.sb("spread", [P, NT, P], BF16)
        ss = m.sb("spread_stage", [P, NT, P])
        an = m.sb("attnT_normed", [P, KC, TILE])
        ah = m.sb("attnT_hi", [P, 2, KC, TILE], F32R)
        al = m.sb("attnT_lo", [P, 2, KC, TILE], F32R)
        xt = m.sb("x", [P, 2, SUB, D])
        zn = m.sb("z_normed", [P, SUB, D])
        x1 = m.sb("x1", [P, 2, SUB, D])
        xn = m.sb("x1_normed", [P, SUB, D])
        xh = m.sb("xT_hi", [P, 2, KC, TILE], F32R)
        xl = m.sb("xT_lo", [P, 2, KC, TILE], F32R)
        ws = m.sb("w_stage", [P, KC, D + NE])
        wh = m.sb("w_hi", [P, KC, D + NE], F32R)
        wl = m.sb("w_lo", [P, KC, D + NE], F32R)
        ones = m.sb("ones", [P, P], F32R)
        bs = m.sb("bias_stage", [P, D])
        bb = m.sb("bias_out", [P, D], F32R)
        eb = m.sb("bias_expert", [P, PAIR, NE])
        ident = m.sb("ident", [P, P])
        spare = m.sb("spare", [P, 1])
        th = m.sb("tanh", [P, PAIR, NE])
        sc = m.sb("scores", [P, PAIR, NE])
        sel = m.sb("scores_biased", [P, PAIR, NE])
        top = m.sb("top8", [P, PAIR, TOPK])
        rest = m.sb("rest", [P, PAIR, NE])
        pick = m.sb("picked", [P, PAIR, NE])
        part = m.sb("picked_scores", [P, PAIR, NE])
        tot = m.sb("picked_sum", [P, PAIR])
        inv = m.sb("picked_inverse", [P, PAIR])
        ps_i = m.ps("ps_inverses", [P, KC, TILE])
        ps_z = m.ps("ps_z", [P, SUB, D])
        ps_x = m.ps("ps_xT", [P, KC, TILE])
        ps_r = m.ps("ps_router", [P, SUB, NE])

        s_w, s_bz, s_b, s_wh, s_wl = (m.sem(n) for n in ("weights_loaded", "bias_zeros", "bias_loaded", "w_hi", "w_split"))
        s_den, s_sp, s_spread, s_inv = (m.sem(n) for n in ("den_loaded", "spread_loaded", "spread_bf", "inverses"))
        z_norm, x_norm = Norm(m, "norm_z"), Norm(m, "norm_x1")
        s_la = [m.sem(f"attn_loaded{i}") for i in range(2)]
        s_lx = [m.sem(f"x_loaded{i}") for i in range(2)]
        s_i, s_an, s_ah, s_al, s_z, s_x1 = (m.sem(n) for n in (
            "inverses_spread", "attnT_normed", "attnT_hi", "attnT_split", "z", "x1_done"))
        s_xT, s_xh, s_xl, s_r = (m.sem(n) for n in ("transposed", "xT_hi", "xT_split", "router_product"))
        s_th, s_sc, s_sel, s_top, s_rest, s_pick, s_part, s_tot, s_ti, s_c = (m.sem(n) for n in (
            "tanh", "scores", "biased", "top8", "rest", "picked", "picked_scores", "picked_sum", "sum_inverse", "combine"))
        s_eh, s_el = m.sem("shared_w_hi"), m.sem("shared_w_split")
        s_sx, s_sT = ([m.sem(f"{n}_stored{i}") for i in range(2)] for n in ("x1", "xT"))

        def there(t):
            return not isinstance(t, int) or 0 <= t < NT

        def steps(eng, step):
            for t in range(-AHEAD, LAG):
                step(t, t % 2)
            pairs = (NT - AHEAD - LAG) // 2
            with eng.Fori(0, pairs) as it:
                for r in range(2):
                    step(it * 2 + LAG + r, (LAG + r) % 2)
            for t in range(LAG + 2 * pairs, NT + LAG):
                step(t, t % 2)

        with nc.Block() as block:

            @block.sync
            def _(sp):
                def load_attn(t, r):
                    half = t % 2 if isinstance(t, int) else r
                    base = t // 2 * D if isinstance(t, int) else (t - half) * (D // 2)
                    sp.dma_start(at[:, r], a_dram[bass.ds(base, D), half * TILE:(half + 1) * TILE].rearrange(
                        "(c p) n -> p c n", p=P)).then_inc(s_la[r], 16)

                def load_x(t, r):
                    sp.dma_start(xt[:, r], x[bass.ds(t * TILE, TILE), :].rearrange("(s p) d -> p s d", p=P)
                                 ).then_inc(s_lx[r], 16)

                sp.dma_start(den[:], den_dram).then_inc(s_den, 16)
                load_attn(0, 0)
                sp.dma_start(ss[:].rearrange("p t m -> p (t m)"), spread_in).then_inc(s_sp, 16)
                sp.dma_start(ws[:, :, 0:D], w2.rearrange("(c p) f -> p c f", p=P)).then_inc(s_w, 16)
                sp.dma_start(ws[:, :, D:D + NE], gate.rearrange("(c p) f -> p c f", p=P)).then_inc(s_w, 16)
                sp.dma_start(eb[:].rearrange("p s e -> p (s e)"), ebias).then_inc(s_w, 16)
                sp.dma_start(ident[:], ident_in).then_inc(s_w, 16)
                sp.wait_ge(s_bz, BASE + 1)
                for row in (0, 32):
                    sp.dma_start(bs[row:row + 1], b2[0:1, :]).then_inc(s_b, 16)
                load_attn(1, 1)
                load_x(0, 0)
                load_x(1, 1)

                def step(t, r):
                    if there(t + 4) and not (isinstance(t, int) and t + 4 < 2):
                        sp.wait_ge(s_an, BASE + t + 3)
                        load_attn(t + 4, r)
                    if isinstance(t, int) and t == NT - 2:
                        for i in range(2):
                            sp.wait_ge(s_sT[i], BASE + 32 * GT // 2)
                        for tt in range(GT):
                            for hl, dst in enumerate((exh, exl)):
                                sp.dma_start(dst[:, tt].bitcast(F32), xT_dram[tt, hl]).then_inc(s_ex[tt], 16)
                    if there(t - 1):
                        sp.wait_ge(s_xl, BASE + t)
                        for hl, src in enumerate((xh, xl)):
                            sp.dma_start(xT_dram[bass.ds(t - 1, 1), hl].rearrange("o p c n -> p (o c) n"),
                                         src[:, 1 - r].bitcast(F32)).then_inc(s_sT[1 - r], 16)
                    if there(t):
                        sp.wait_ge(s_x1, BASE + t + 1)
                        if there(t + 2):
                            load_x(t + 2, r)
                        sp.dma_start(x1_dram[bass.ds(t, 1)].rearrange("o p s d -> p (o s) d"), x1[:, r]).then_inc(s_sx[r], 16)

                steps(sp, step)
                for r in range(2):
                    sp.wait_ge(s_sx[r], BASE + 16 * NT // 2)
                    sp.wait_ge(s_sT[r], BASE + 32 * NT // 2)

            @block.gpsimd
            def _(pool):
                m.lift(pool)
                pool.memset(bs[:], 0.0).then_inc(s_bz, 1)
                pool.dma_start(ews[:, 0], w_sh).then_inc(s_ews[0], 16)
                pool.dma_start(ews[:, 1], w_exp[0]).then_inc(s_ews[1], 16)
                z_norm.constants(pool)
                x_norm.constants(pool)

                def step(t, r):
                    if there(t + 1):
                        z_norm.root(pool, t + 1)
                    if there(t):
                        x_norm.root(pool, t)
                    if there(t + 1):
                        pool.wait_ge(s_lx[1 - r], BASE + 16 * half_count(t + 1, 1 - r))
                        pool.wait_ge(z_norm.done, BASE + t + 2)
                        if there(t - 1):
                            pool.wait_ge(s_sx[1 - r], BASE + 16 * half_count(t - 1, 1 - r))
                        pool.tensor_tensor(x1[:, 1 - r], xt[:, 1 - r], zn[:], ALU.add).then_inc(s_x1, 1)

                steps(pool, step)

            @block.vector
            def _(dve):
                dve.wait_ge(s_den, BASE + 16)
                for half in range(2):
                    cols = slice(half * TILE, (half + 1) * TILE)
                    dve.reciprocal(den[:, cols], den[:, cols]).then_inc(s_inv, 1)
                    for n, part_of in enumerate((den, rem, rem)):
                        dve.wait_ge(s_inv, BASE + 6 * half + 2 * n + 1)
                        dve.tensor_copy(dp[:, n, cols], part_of[:, cols]).then_inc(s_inv, 1)
                        if n < 2:
                            dve.wait_ge(s_inv, BASE + 6 * half + 2 * n + 2)
                            dve.tensor_tensor(rem[:, cols], part_of[:, cols], dp[:, n, cols], ALU.subtract
                                              ).then_inc(s_inv, 1)
                dve.wait_ge(s_w, BASE + 64)
                dve.tensor_scalar(ones[:], ident[:], 0.0, 1.0, ALU.mult, ALU.add).then_inc(s_wl, 1)
                dve.wait_ge(s_wh, BASE + 1)
                dve.tensor_tensor(wl[:], ws[:], wh[:].bitcast(F32), ALU.subtract).then_inc(s_wl, 1)
                dve.wait_ge(s_wh, BASE + 2)
                dve.tensor_tensor(bb[32:33], bs[32:33], bb[32:33].bitcast(F32), ALU.subtract).then_inc(s_wl, 1)

                def scale_attn(t, r):
                    dve.wait_ge(s_la[r], BASE + 16 * half_count(t, r))
                    dve.wait_ge(s_i, BASE + t + 1)
                    dve.wait_ge(s_al, BASE + t)
                    dve.tensor_tensor(an[:], at[:, r], ps_i[:], ALU.mult).then_inc(s_an, 1)

                def split_x(t, r):
                    dve.wait_ge(s_xh, BASE + t + 1)
                    dve.tensor_tensor(xl[:, r], ps_x[:], xh[:, r].bitcast(F32), ALU.subtract).then_inc(s_xl, 1)

                def route(t):
                    pair = t // 2
                    dve.wait_ge(s_th, BASE + t + 2)
                    dve.tensor_scalar(sc[:], th[:], 0.5, 0.5, ALU.mult, ALU.add).then_inc(s_sc, 1)
                    dve.wait_ge(s_sc, BASE + pair + 1)
                    dve.tensor_tensor(sel[:], sc[:], eb[:], ALU.add).then_inc(s_sel, 1)
                    dve.wait_ge(s_sel, BASE + pair + 1)
                    dve.memset(spare[:], 0.0)
                    for s in range(PAIR):
                        last = dve.max(top[:, s], sel[:, s])
                    last.then_inc(s_top, 1)
                    dve.wait_ge(s_top, BASE + pair + 1)
                    dve.memset(spare[:], 0.0)
                    for s in range(PAIR):
                        last = dve.match_replace(rest[:, s], top[:, s], sel[:, s], -1e30)
                    last.then_inc(s_rest, 1)
                    dve.wait_ge(s_rest, BASE + pair + 1)
                    dve.tensor_tensor(pick[:], rest[:], sel[:], ALU.not_equal).then_inc(s_pick, 1)
                    dve.wait_ge(s_pick, BASE + pair + 1)
                    dve.tensor_tensor(part[:], pick[:], sc[:], ALU.mult).then_inc(s_part, 1)
                    dve.wait_ge(s_part, BASE + pair + 1)
                    dve.tensor_reduce(tot[:], part[:], AX.X, ALU.add).then_inc(s_tot, 1)
                    dve.wait_ge(s_tot, BASE + pair + 1)
                    dve.reciprocal(inv[:], tot[:]).then_inc(s_ti, 1)
                    dve.wait_ge(s_ti, BASE + pair + 1)
                    dve.scalar_tensor_tensor(combine[:, bass.ds(t * SUB, PAIR), :], part[:], ROUTE_SCALE,
                                             inv[:].rearrange("p (s o) -> p s o", o=1).broadcast_to((P, PAIR, NE)),
                                             ALU.mult, ALU.mult).then_inc(s_c, 1)

                def step(t, r):
                    if there(t + 3):
                        scale_attn(t + 3, 1 - r)
                    if there(t + 1):
                        dve.wait_ge(s_z, BASE + t + 2)
                        z_norm.moments(dve, t + 1, lambda s: ps_z[:, s])
                    if there(t):
                        dve.wait_ge(s_x1, BASE + t + 1)
                        x_norm.moments(dve, t, lambda s: x1[:, r, s])
                    if there(t - 1):
                        if there(t - 3):
                            dve.wait_ge(s_sT[1 - r], BASE + 32 * half_count(t - 3, 1 - r))
                            dve.wait_ge(s_r, BASE + t - 2)
                        split_x(t - 1, 1 - r)
                    if there(t + 3):
                        dve.wait_ge(s_ah, BASE + t + 4)
                        dve.tensor_tensor(al[:, 1 - r], an[:], ah[:, 1 - r].bitcast(F32), ALU.subtract).then_inc(s_al, 1)
                    if r == 1 and there(t - 3):
                        route(t - 3)
                    if isinstance(t, int) and t == NT - 1:
                        dve.wait_ge(s_eh, BASE + 1)
                        dve.tensor_tensor(ewl[:, 0], ews[:, 0], ewh[:, 0].bitcast(F32), ALU.subtract).then_inc(s_el, 1)

                steps(dve, step)

            @block.scalar
            def _(act):
                act.wait_ge(s_sp, BASE + 16)
                act.activation(spread[:], ss[:], ACT.Copy).then_inc(s_spread, 1)
                act.wait_ge(s_w, BASE + 64)
                act.activation(wh[:], ws[:], ACT.Copy).then_inc(s_wh, 1)
                act.wait_ge(s_b, BASE + 32)
                act.activation(bb[:], bs[:], ACT.Copy).then_inc(s_wh, 1)

                def step(t, r):
                    if there(t - 2):
                        act.wait_ge(s_r, BASE + t - 1)
                        if r == 0:
                            act.wait_ge(s_sc, BASE + (t - 2) // 2)
                        act.activation(th[:, r * SUB:(r + 1) * SUB], ps_r[:], ACT.Tanh, scale=0.5).then_inc(s_th, 1)
                    if there(t + 3):
                        act.wait_ge(s_an, BASE + t + 4)
                        act.wait_ge(s_z, BASE + t + 2)
                        act.activation(ah[:, 1 - r], an[:], ACT.Copy).then_inc(s_ah, 1)
                    if there(t + 1):
                        act.wait_ge(s_x1, BASE + t + 1)
                        z_norm.apply(act, t + 1, lambda s: ps_z[:, s], lambda s: zn[:, s])
                    if there(t):
                        act.wait_ge(s_xT, BASE + t)
                        x_norm.apply(act, t, lambda s: x1[:, r, s], lambda s: xn[:, s])
                    if there(t):
                        act.wait_ge(s_xT, BASE + t + 1)
                        if there(t - 2):
                            act.wait_ge(s_sT[r], BASE + 32 * half_count(t - 2, r))
                        act.activation(xh[:, r], ps_x[:], ACT.Copy).then_inc(s_xh, 1)

                    if isinstance(t, int) and t == NT - 2:
                        act.wait_ge(s_ews[0], 16)
                        act.activation(ewh[:, 0], ews[:, 0], ACT.Copy).then_inc(s_eh, 1)

                steps(act, step)

            @block.tensor
            def _(pe):
                pe.wait_ge(s_spread, BASE + 1)

                def spread_inverses(t, half):
                    if isinstance(t, int) and t < 2:
                        pe.wait_ge(s_inv, BASE + 6 * (t + 1))
                    pe.wait_ge(s_an, BASE + t)
                    for c in range(KC):
                        for n in range(3):
                            last = pe.matmul(ps_i[:, c], spread[:, bass.ds(t - half + c, 1)].rearrange("p o m -> p (o m)"),
                                             dp[:, n, half * TILE:(half + 1) * TILE], start=n == 0, stop=n == 2)
                    last.then_inc(s_i, 1)

                def project(t, r):
                    pe.wait_ge(s_al, BASE + t + 1)
                    pe.wait_ge(z_norm.done, BASE + t)
                    for s in range(SUB):
                        tok = slice(s * P, (s + 1) * P)
                        pe.matmul(ps_z[:, s], ones[:], bb[:], start=True, stop=False)
                        for c in range(KC):
                            a_hi, a_lo = ah[:, r, c, tok], al[:, r, c, tok]
                            w_hi, w_lo = wh[:, c, 0:D], wl[:, c, 0:D]
                            pe.matmul(ps_z[:, s], a_hi, w_hi, start=False, stop=False)
                            pe.matmul(ps_z[:, s], a_hi, w_lo, start=False, stop=False)
                            last = pe.matmul(ps_z[:, s], a_lo, w_hi, start=False, stop=c == KC - 1)
                    last.then_inc(s_z, 1)

                def transposes(t):
                    pe.wait_ge(x_norm.done, BASE + t + 1)
                    pe.wait_ge(s_xl, BASE + t)
                    for c in range(KC):
                        for s in range(SUB):
                            last = pe.transpose(ps_x[:, c, s * P:(s + 1) * P], xn[:, s, c * P:(c + 1) * P], ident[:])
                    last.then_inc(s_xT, 1)

                def router(t, r):
                    pe.wait_ge(s_xl, BASE + t + 1)
                    pe.wait_ge(s_th, BASE + t)
                    for s in range(SUB):
                        tok = slice(s * P, (s + 1) * P)
                        last = three_products(pe, ps_r[:, s], lambda c: xh[:, r, c, tok], lambda c: xl[:, r, c, tok],
                                              lambda c: wh[:, c, D:D + NE], lambda c: wl[:, c, D:D + NE], KC)
                    last.then_inc(s_r, 1)

                def step(t, r):
                    if there(t - 2):
                        router(t - 2, r)
                    if there(t + 4):
                        spread_inverses(t + 4, r)
                    if there(t + 2):
                        if isinstance(t, int) and t + 2 == 0:
                            pe.wait_ge(s_wl, BASE + 3)
                        project(t + 2, r)
                    if there(t):
                        transposes(t)

                steps(pe, step)


def experts(nc, outer, w_exp, w_sh, weights, tiles, x1_dram, xT_dram, combine, out):
    with ExitStack() as inner:
        m = Mem(nc, outer, inner, "D")
        one = m.sb("one", [P, 1])
        ws, wh, wl, s_ws = weights
        xh, xl, s_x = tiles
        x1 = m.sb("x1", [P, GT, SUB, D])
        y = m.sb("y", [P, GT, SUB, D])
        yn = m.sb("y_normed", [P, SUB, D])
        ob = m.sb("out", [P, 2, SUB, D])
        th = m.sb("tanh", [P, KC, TILE])
        v = m.sb("gated", [P, KC, TILE])
        h = m.sb("hidden", [P, 2, KC, TILE])
        hh = m.sb("hidden_hi", [P, 2, KC, TILE], F32R)
        hl = m.sb("hidden_lo", [P, 2, KC, TILE], F32R)
        ps_g = m.ps("ps_gate", [P, KC, TILE])
        ps_u = m.ps("ps_up", [P, KC, TILE])
        ps_y = m.ps("ps_y", [P, 2, SUB, D])

        NW = NE + 1
        s_wh, s_wl, s_one = m.sem("w_hi"), m.sem("w_split"), m.sem("one")
        norm = Norm(m, "norm_y", lead=GT)
        s_x1 = [m.sem(f"x1_loaded{i}") for i in range(GT)]
        s_gu, s_th, s_v, s_h, s_hh, s_hl = (m.sem(n) for n in (
            "hidden_products", "tanh", "gated", "hidden", "hidden_hi", "hidden_split"))
        s_yp, s_acc, s_ob = m.sem("y_products"), m.sem("accumulated"), m.sem("out_done")
        s_st = [m.sem(f"out_stored{i}") for i in range(2)]

        with nc.Block() as block:

            @block.sync
            def _(sp):
                def load_x1(g, tt):
                    sp.dma_start(x1[:, tt], x1_dram[bass.ds(g * GT + tt, 1)].rearrange("o p s d -> p (o s) d")
                                 ).then_inc(s_x1[tt], 16)

                for tt in range(GT):
                    load_x1(0, tt)

                def step(g, more):
                    for tt in range(GT):
                        sp.wait_ge(s_ob, BASE + g * GT + tt + 1)
                        sp.dma_start(out[bass.ds((g * GT + tt) * TILE, TILE), :].rearrange("(s p) d -> p s d", p=P),
                                     ob[:, tt % 2]).then_inc(s_st[tt % 2], 16)
                        if more:
                            load_x1(g + 1, tt)

                with sp.Fori(0, NGR - 1) as g:
                    step(g, True)
                step(NGR - 1, False)
                for i in range(2):
                    sp.wait_ge(s_st[i], BASE + 16 * NT // 2)

            @block.gpsimd
            def _(pool):
                def load(e, r):
                    src = w_sh if e is None else w_exp[bass.ds(e, 1)].rearrange("o p a c n -> p (o a) c n")
                    pool.dma_start(ws[:, r], src).then_inc(s_ws[r], 16)

                def split(w, r, first):
                    pool.wait_ge(s_ws[r], 16 * ((w - r) // 2 + 1))
                    if not first:
                        pool.wait_ge(s_yp, BASE + GT * (w - 1))
                    for a in range(3):
                        pool.tensor_tensor(wh[:, r, a].rearrange("p c n -> p (c n)"),
                                           ws[:, r, a].rearrange("p c n -> p (c n)"),
                                           one[:].broadcast_to((P, KC * D)), ALU.mult).then_inc(s_wh, 1)
                        pool.wait_ge(s_wh, BASE + 3 * w + a + 1)
                        pool.tensor_tensor(wl[:, r, a], ws[:, r, a], wh[:, r, a].bitcast(F32), ALU.subtract
                                           ).then_inc(s_wl, 1)
                    pool.wait_ge(s_wl, BASE + 3 * w + 3)

                def finish(g):
                    for tt in range(GT):
                        t = g * GT + tt
                        norm.root(pool, t)
                        pool.wait_ge(norm.done, BASE + norm.lead + t + 1)
                        pool.wait_ge(s_x1[tt], BASE + 16 * (g + 1))
                        pool.wait_ge(s_st[tt % 2], BASE + 16 * (g * 2 + tt // 2))
                        pool.tensor_tensor(ob[:, tt % 2], x1[:, tt], yn[:], ALU.add).then_inc(s_ob, 1)

                m.lift(pool)
                pool.sem_inc(norm.done, norm.lead)
                pool.sem_inc(s_wh, 3)
                pool.sem_inc(s_wl, 3)
                norm.constants(pool)
                pool.memset(one[:], 1.0).then_inc(s_one, 1)
                pool.wait_ge(s_one, BASE + 1)
                for g in range(NGR):
                    w = g * NW
                    if g > 0:
                        split(w, w % 2, False)
                    load(1, w % 2)
                    if g > 0:
                        finish(g - 1)
                    split(w + 1, (w + 1) % 2, w + 1 < 2)
                    load(2, (w + 1) % 2)
                    with pool.Fori(0, (NE - 4) // 2) as it:
                        for k in range(2):
                            r = (w + 2 + k) % 2
                            split(it * 2 + (w + 2 + k), r, False)
                            load(it * 2 + (3 + k), r)
                    for e in range(NE - 3, NE):
                        r = (w + 1 + e) % 2
                        split(w + 1 + e, r, False)
                        if e + 2 < NE:
                            load(e + 2, r)
                        elif g + 1 < NGR:
                            load(None if e + 2 == NE else 0, r)
                finish(NGR - 1)

            @block.vector
            def _(dve):

                def gate(n, tt):
                    r = tt % 2
                    for k in range(KC):
                        dve.wait_ge(s_th, BASE + KC * n + k + 1)
                        dve.scalar_tensor_tensor(v[:, k], th[:, k], 1.0, ps_g[:, k], ALU.add, ALU.mult).then_inc(s_v, 1)
                        dve.wait_ge(s_v, BASE + KC * n + k + 1)
                        dve.scalar_tensor_tensor(h[:, r, k], v[:, k], 0.5, ps_u[:, k], ALU.mult, ALU.mult
                                                 ).then_inc(s_h, 1)

                def low(n, tt):
                    r = tt % 2
                    for k in range(KC):
                        dve.wait_ge(s_hh, BASE + KC * n + k + 1)
                        dve.tensor_tensor(hl[:, r, k], h[:, r, k], hh[:, r, k].bitcast(F32), ALU.subtract
                                          ).then_inc(s_hl, 1)

                def accumulate(n, g, e, tt):
                    dve.wait_ge(s_yp, BASE + n + 1)
                    if e is None:
                        dve.wait_ge(norm.done, BASE + g * GT + tt + 1)
                        last = dve.tensor_copy(y[:, tt], ps_y[:, tt % 2])
                    else:
                        dve.wait_ge(s_acc, BASE + n - GT + 1)
                        for s in range(SUB):
                            c = combine[:, bass.ds((g * GT + tt) * SUB + s, 1), bass.ds(e, 1)].rearrange(
                                "p a b -> p (a b)")
                            last = dve.scalar_tensor_tensor(y[:, tt, s], ps_y[:, tt % 2, s], c, y[:, tt, s],
                                                            ALU.mult, ALU.add)
                    last.then_inc(s_acc, 1)

                def moments(g, tt):
                    dve.wait_ge(s_acc, BASE + (g * NW + NE) * GT + tt + 1)
                    norm.moments(dve, g * GT + tt, lambda s: y[:, tt, s])

                def ahead(n, tt, more=True):
                    if more:
                        gate(n + 1, (tt + 1) % GT)
                        low(n + 1, (tt + 1) % GT)

                def group(g, more):
                    for tt in range(GT):
                        n = g * (NW * GT) + tt
                        ahead(n, tt)
                        accumulate(n, g, None, tt)
                    with dve.Fori(0, NE - 1) as e:
                        for tt in range(GT):
                            n = g * (NW * GT) + (e + 1) * GT + tt
                            ahead(n, tt)
                            accumulate(n, g, e, tt)
                    for tt in range(GT):
                        n = g * (NW * GT) + NE * GT + tt
                        ahead(n, tt, more or tt < GT - 1)
                        accumulate(n, g, NE - 1, tt)
                        moments(g, tt)

                gate(0, 0)
                low(0, 0)
                with dve.Fori(0, NGR - 1) as g:
                    group(g, True)
                group(NGR - 1, False)

            @block.scalar
            def _(act):
                def load_x(g, tt):
                    for hl_, dst in enumerate((xh, xl)):
                        act.dma_start(dst[:, tt].bitcast(F32), xT_dram[bass.ds(g * GT + tt, 1), hl_].rearrange(
                            "o p c n -> p (o c) n")).then_inc(s_x[tt], 16)

                def tanh_and_hi(n, tt):
                    for k in range(KC):
                        act.wait_ge(s_gu, BASE + KC * n + k + 1)
                        act.wait_ge(s_v, BASE + KC * n)
                        act.activation(th[:, k], ps_g[:, k], ACT.Tanh, scale=0.5).then_inc(s_th, 1)
                    for k in range(KC):
                        act.wait_ge(s_h, BASE + KC * n + k + 1)
                        act.activation(hh[:, tt % 2, k], h[:, tt % 2, k], ACT.Copy).then_inc(s_hh, 1)

                def normed(g, tt):
                    act.wait_ge(s_ob, BASE + g * GT + tt)
                    norm.apply(act, g * GT + tt, lambda s: y[:, tt, s], lambda s: yn[:, s])

                def group(g, more):
                    first = g * (NW * GT) + 2
                    with act.Fori(0, NE) as e:
                        for tt in range(GT):
                            tanh_and_hi(first + e * GT + tt, (tt + 2) % GT)
                    for tt in range(GT):
                        if more:
                            load_x(g + 1, tt)
                        if more or tt < GT - 2:
                            tanh_and_hi(first + NE * GT + tt, (tt + 2) % GT)
                        normed(g, tt)

                tanh_and_hi(0, 0)
                tanh_and_hi(1, 1)
                with act.Fori(0, NGR - 1) as g:
                    group(g, True)
                group(NGR - 1, False)

            @block.tensor
            def _(pe):
                def hidden(n, w, r, tt):
                    if tt == 0:
                        pe.wait_ge(s_wl, BASE + 3 * w + 3)
                    pe.wait_ge(s_x[tt], 32 * (w // NW + 1))
                    pe.wait_ge(s_h, BASE + KC * n)
                    for k in range(KC):
                        cols = slice(k * P, (k + 1) * P)
                        for a, o in ((0, ps_g), (1, ps_u)):
                            last = three_products(pe, o[:, k], lambda c: wh[:, r, a, c, cols],
                                                  lambda c: wl[:, r, a, c, cols], lambda c: xh[:, tt, c],
                                                  lambda c: xl[:, tt, c], KC)
                        last.then_inc(s_gu, 1)

                def down(n, r, tt):
                    pe.wait_ge(s_hl, BASE + KC * n + KC)
                    if tt >= 2:
                        pe.wait_ge(s_acc, BASE + n - 1)
                    else:
                        pe.wait_ge(s_acc, BASE + n - tt)
                    b = tt % 2
                    for s in range(SUB):
                        tok = slice(s * P, (s + 1) * P)
                        last = three_products(pe, ps_y[:, b, s], lambda c: hh[:, b, c, tok], lambda c: hl[:, b, c, tok],
                                              lambda c: wh[:, r, 2, c], lambda c: wl[:, r, 2, c], KC)
                    last.then_inc(s_yp, 1)

                def expert(w, r, more):
                    for tt in range(GT):
                        n = w * GT + tt
                        if tt < GT - 1:
                            hidden(n + 1, w, r, tt + 1)
                        elif more:
                            hidden(n + 1, w + 1, 1 - r, 0)
                        down(n, r, tt)

                hidden(0, 0, 0, 0)
                with pe.Fori(0, NGR * NW // 2 - 1) as it:
                    for r in range(2):
                        expert(it * 2 + r, r, True)
                expert(NGR * NW - 2, 0, True)
                expert(NGR * NW - 1, 1, False)


def build(nc, x, w1, b1c, b1v, w2, b2, gate, ebias, w_exp, w_sh, ident, mask, maskT, spread, out):
    qk = nc.dram_tensor("qk_scratch", (2, 2, B * D, S), F32, kind="Internal").ap()
    v = nc.dram_tensor("v_scratch", (T, D), F32, kind="Internal").ap()
    attn = nc.dram_tensor("attn_scratch", (B * D, S), F32, kind="Internal").ap()
    den = nc.dram_tensor("den_scratch", (B * H, S), F32, kind="Internal").ap()
    x1 = nc.dram_tensor("x1_scratch", (NT, P, SUB, D), F32, kind="Internal").ap()
    xT = nc.dram_tensor("xT_scratch", (NT, 2, P, KC, TILE), F32, kind="Internal").ap()
    with ExitStack() as outer:
        combine = outer.enter_context(nc.sbuf_tensor("combine", [P, NT * SUB, NE], F32))
        project_qkv(nc, outer, x, w1, b1c, b1v, ident, qk, v)
        attention(nc, outer, ident, mask, maskT, qk, v, attn, den)
        weights = [outer.enter_context(nc.sbuf_tensor(f"expert_w_{n}", [P, 2, 3, KC, D], dt))
                   for n, dt in (("stage", F32), ("hi", F32R), ("lo", F32R))]
        weights.append([outer.enter_context(nc.semaphore(f"expert_w_loaded{i}")) for i in range(2)])
        tiles = [outer.enter_context(nc.sbuf_tensor(f"expert_xT_{n}", [P, GT, KC, TILE], F32R)) for n in ("hi", "lo")]
        tiles.append([outer.enter_context(nc.semaphore(f"expert_xT_loaded{i}")) for i in range(GT)])
        output_and_route(nc, outer, x, w2, b2, gate, ebias, ident, spread, attn, den, x1, xT, combine, w_exp, w_sh,
                         weights, tiles)
        experts(nc, outer, w_exp, w_sh, weights, tiles, x1, xT, combine, out)


def kernel(L0_attn_x, L0_attn_W1, L0_attn_b1, L0_attn_W2, L0_attn_b2, L0_ffn_gate_w, L0_ffn_expert_bias,
           L0_ffn_w_gate, L0_ffn_w_up, L0_ffn_w_down, L0_ffn_shared_gate_w, L0_ffn_shared_up_w,
           L0_ffn_shared_down_w):
    import concourse.bacc as bacc
    from concourse.bass_utils import run_bass_kernel_spmd

    def rows(a):
        return np.broadcast_to(np.asarray(a)[None, :], (P, a.shape[-1]))

    def apart(a):
        return a.reshape(*a.shape[:-2], KC, P, a.shape[-1]).swapaxes(-3, -2)

    def weights(g, u, d):
        return np.stack([apart(np.swapaxes(w, -1, -2)) for w in map(np.asarray, (g, u, d))], axis=-4).swapaxes(-4, -3)

    w1 = np.asarray(L0_attn_W1).reshape(D, H, 3, DH).transpose(0, 2, 1, 3).reshape(D, 3 * D)
    b1 = np.asarray(L0_attn_b1).reshape(H, 3, DH).transpose(1, 0, 2).reshape(3 * D)
    i = np.arange(P)
    arrays = {
        "x": np.asarray(L0_attn_x).reshape(T, D), "w1": w1, "b1c": b1[:2 * D].reshape(4, P).T, "b1v": rows(b1[2 * D:]),
        "w2": np.asarray(L0_attn_W2), "b2": rows(L0_attn_b2), "gate": np.asarray(L0_ffn_gate_w).T,
        "ebias": rows(np.tile(np.asarray(L0_ffn_expert_bias), 2 * SUB)), "w_exp": weights(L0_ffn_w_gate, L0_ffn_w_up, L0_ffn_w_down),
        "w_sh": weights(L0_ffn_shared_gate_w, L0_ffn_shared_up_w, L0_ffn_shared_down_w),
        "ident": np.eye(P, dtype=np.float32),
        "mask": np.where(i[None, :] > i[:, None], MASK, 0.0).astype(np.float32),
        "maskT": np.where(i[None, :] < i[:, None], MASK, 0.0).astype(np.float32),
        "spread": np.repeat(np.eye(P, dtype=np.float32), DH, axis=1),
    }
    arrays = {f"in_{k}": np.ascontiguousarray(a) for k, a in arrays.items()}
    nc = bacc.Bacc("TRN2", target_bir_lowering=False, num_devices=1)
    aps = [nc.dram_tensor(k, a.shape, mybir.dt.from_np(a.dtype), kind="ExternalInput").ap() for k, a in arrays.items()]
    out = nc.dram_tensor("out", (T, D), F32, kind="ExternalOutput").ap()
    build(nc, *aps, out)
    got = run_bass_kernel_spmd(nc, [arrays], core_ids=[0]).results[0]["out"]
    return got.reshape(B, S, D)
```
